# Optimizing a Trainium2 kernel written in Bass

```python
import numpy as np
import jax
import jax.numpy as jnp

def _softmax(x, axis=-1):
    return jax.nn.softmax(x, axis=axis)

def _gelu(x):
    return jax.nn.gelu(x, approximate=True)

def _silu(x):
    return jax.nn.silu(x)

def _sigmoid(x):
    return jax.nn.sigmoid(x)

def _layernorm(x, axis=-1, eps=1e-05):
    m = jnp.mean(x, axis=axis, keepdims=True)
    v = jnp.var(x, axis=axis, keepdims=True)
    return (x - m) / jnp.sqrt(v + eps)

def _scatter_add(tgt, idx, src, axis=0):
    return tgt.at[idx].add(src)

def _segment_sum(src, seg, n):
    return jax.ops.segment_sum(src, seg, n)
kernel_name = 'mk_gnn_preln_d1_gnn_r32_bec49b'

def setup_inputs(seed: int=0):
    np.random.seed(seed)
    _w = jnp.asarray

    def _rec_inputs():
        import jax
        import jax.numpy as jnp
        _gk = jax.random.key(seed)
        x = -0.0006008 + 1.001 * jax.random.normal(jax.random.fold_in(_gk, 1), (50000, 256), jnp.float32)
        src = jax.random.randint(jax.random.fold_in(_gk, 2), (50000,), 0, 50000, jnp.int32)
        dst = jax.random.randint(jax.random.fold_in(_gk, 3), (50000,), 0, 50000, jnp.int32)
        _o = jnp.argsort(dst, stable=True)
        src = src[_o]
        dst = dst[_o]
        edge_type_2 = jax.random.randint(jax.random.fold_in(_gk, 12), (50000,), 0, 2, jnp.int32)
        return (x, src, dst, edge_type_2)
    x, src, dst, edge_type_2 = _rec_inputs()

    def _L0_gnn_setup():
        import jax, jax.numpy as jnp
        import numpy as np
        N_NODES = 10000
        N_EDGES = 10000
        D = 256
        D_OUT = 256
        NUM_REL = 2
        key = jax.random.key(seed)
        ks = jax.random.split(key, 16)
        s = 1.0 / np.sqrt(D)
        inp = {}
        inp['feat'] = jax.random.normal(ks[0], (N_NODES, D), dtype=jnp.float32)
        inp['src'] = jax.random.randint(ks[1], (N_EDGES,), 0, N_NODES, dtype=jnp.int32)
        inp['dst'] = jax.random.randint(ks[2], (N_EDGES,), 0, N_NODES, dtype=jnp.int32)
        inp['rel'] = jax.random.randint(ks[3], (N_EDGES,), 0, NUM_REL, dtype=jnp.int32)
        inp['W_rel'] = jax.random.normal(ks[4], (NUM_REL, D, D), dtype=jnp.float32) * s
        inp['b_rel'] = jax.random.normal(ks[5], (NUM_REL, D), dtype=jnp.float32) * s
        inp['W_ih'] = jax.random.normal(ks[6], (4 * D, D), dtype=jnp.float32) * s
        inp['b_ih'] = jax.random.normal(ks[7], (4 * D,), dtype=jnp.float32) * s
        inp['b_hh'] = jax.random.normal(ks[8], (4 * D,), dtype=jnp.float32) * s
        h = D // 2
        inp['W1'] = jax.random.normal(ks[9], (h, D), dtype=jnp.float32) * s
        inp['b1'] = jax.random.normal(ks[10], (h,), dtype=jnp.float32) * s
        inp['W2'] = jax.random.normal(ks[11], (h, h), dtype=jnp.float32) * (1.0 / np.sqrt(h))
        inp['b2'] = jax.random.normal(ks[12], (h,), dtype=jnp.float32) * (1.0 / np.sqrt(h))
        inp['W3'] = jax.random.normal(ks[13], (D_OUT, h), dtype=jnp.float32) * (1.0 / np.sqrt(h))
        inp['b3'] = jax.random.normal(ks[14], (D_OUT,), dtype=jnp.float32) * (1.0 / np.sqrt(h))
        return inp
    _L0_gnn_all = _L0_gnn_setup()
    _L0_gnn_in = {k: v for k, v in _L0_gnn_all.items() if k in ('W_rel', 'b_rel', 'W_ih', 'b_ih', 'b_hh', 'W1', 'b1', 'W2', 'b2', 'W3', 'b3')}
    del _L0_gnn_all
    return {'x': x, 'src': src, 'dst': dst, 'edge_type_2': edge_type_2, 'L0_gnn_W_rel': _L0_gnn_in['W_rel'], 'L0_gnn_b_rel': _L0_gnn_in['b_rel'], 'L0_gnn_W_ih': _L0_gnn_in['W_ih'], 'L0_gnn_b_ih': _L0_gnn_in['b_ih'], 'L0_gnn_b_hh': _L0_gnn_in['b_hh'], 'L0_gnn_W1': _L0_gnn_in['W1'], 'L0_gnn_b1': _L0_gnn_in['b1'], 'L0_gnn_W2': _L0_gnn_in['W2'], 'L0_gnn_b2': _L0_gnn_in['b2'], 'L0_gnn_W3': _L0_gnn_in['W3'], 'L0_gnn_b3': _L0_gnn_in['b3']}

def reference(x, src, dst, edge_type_2, L0_gnn_W_rel, L0_gnn_b_rel, L0_gnn_W_ih, L0_gnn_b_ih, L0_gnn_b_hh, L0_gnn_W1, L0_gnn_b1, L0_gnn_W2, L0_gnn_b2, L0_gnn_W3, L0_gnn_b3):
    import jax
    import jax.numpy as jnp

    def _L0_gnn_ref(feat, src, dst, rel, W_rel, b_rel, W_ih, b_ih, b_hh, W1, b1, W2, b2, W3, b3):
        import jax, jax.numpy as jnp
        import numpy as np
        N_NODES = 10000
        N_EDGES = 10000
        D = 256
        D_OUT = 256
        NUM_REL = 2
        n_nodes = feat.shape[0]
        S = feat[src]

        def edge_nn(x, W, b):
            h = jax.nn.relu(x @ W.T + b)
            return jax.nn.relu(h @ W.T + b)
        msgs = jnp.zeros_like(S)
        for r in range(W_rel.shape[0]):
            msgs = jnp.where((rel == r)[:, None], edge_nn(S, W_rel[r], b_rel[r]), msgs)
        agg = jax.ops.segment_sum(msgs, dst, num_segments=n_nodes)
        gates = agg @ W_ih.T + b_ih + b_hh
        i, f, g, o = jnp.split(gates, 4, axis=-1)
        c = jax.nn.sigmoid(i) * jnp.tanh(g)
        hn = jax.nn.sigmoid(o) * jnp.tanh(c)
        x = jax.nn.relu(hn @ W1.T + b1)
        x = jax.nn.relu(x @ W2.T + b2)
        return x @ W3.T + b3
    h = jnp.maximum(_layernorm(x, axis=-1), 0.0)
    x = x + _L0_gnn_ref(h, src, dst, edge_type_2, L0_gnn_W_rel, L0_gnn_b_rel, L0_gnn_W_ih, L0_gnn_b_ih, L0_gnn_b_hh, L0_gnn_W1, L0_gnn_b1, L0_gnn_W2, L0_gnn_b2, L0_gnn_W3, L0_gnn_b3)
    return x

_drawn_inputs = setup_inputs


def setup_inputs(seed=0):
    import zlib

    import numpy as np

    out = dict(_drawn_inputs(seed))
    spreads = {}
    factors = {'L0_gnn_b_rel': 8.0, 'L0_gnn_b_ih': 8.0, 'L0_gnn_b_hh': 8.0}
    for name, (base, spread) in spreads.items():
        noise = np.random.default_rng([zlib.crc32(name.encode()), seed]).standard_normal(out[name].shape)
        drawn = base * np.exp(spread * noise) if base else spread * noise
        out[name] = jnp.asarray(drawn.astype(out[name].dtype))
    for name, factor in factors.items():
        out[name] = (out[name] * factor).astype(out[name].dtype)
    return out
```

```python
import concourse.bass as bass
from concourse import mybir
from contextlib import ExitStack

F32 = mybir.dt.float32
F32R = mybir.dt.float32r
F16 = mybir.dt.float16
I32 = mybir.dt.int32
ALU = mybir.AluOpType
ACT = mybir.ActivationFunctionType

P = 128
D = 256
KH = D // P
NODES = 50000
EDGES = 50000
NUM_REL = 2
LN_EPS = 1e-5

BLOCKS = 4
ROWS = 125
COLS = EDGES // BLOCKS // ROWS
PAIR = 2 * P
BLOCK_PAIRS = (ROWS * COLS + 2 * (PAIR - 1)) // PAIR
BLOCK_TILES = 2 * BLOCK_PAIRS
BLOCK_SLOTS = BLOCK_PAIRS * PAIR
PAIRS = BLOCKS * BLOCK_PAIRS
TILES = 2 * PAIRS
NPAY = 4

SPARE = 65536.0
FAR = 1.0e6

AGG_ROWS = -(-(NODES + PAIR) // P) * P
AGG_PART = AGG_ROWS // P * D
ZERO_REPS = 48
ZERO_W = AGG_PART // ZERO_REPS
assert ZERO_W * ZERO_REPS == AGG_PART
ZERO_DMAS = 6

UNIT = 512
UT = UNIT // P
UNITS = -(-NODES // UNIT)
CHUNKS = 6
CHUNK_ROWS = [0, 512, 768, 128, 640, 896]
RH = D // 2


class At:

    def __init__(self, j, u, unroll):
        self.j, self.u, self.unroll = j, u, unroll

    def __add__(self, off):
        return At(self.j, self.u + off, self.unroll)

    def __sub__(self, off):
        return At(self.j, self.u - off, self.unroll)

    @property
    def n(self):
        return self.j * self.unroll + self.u

    def slot(self, ring):
        assert self.unroll % ring == 0
        return self.u % ring

    def turn(self, ring):
        return self.j * (self.unroll // ring) + self.u // ring

    def within(self, count):
        return not isinstance(self.j, int) or 0 <= self.n < count


def wait_from(eng, sem, value):
    if not isinstance(value, int) or value > 0:
        eng.wait_ge(sem, value)


def run_steps(eng, first, loop_from, loop_to, last, unroll, step):
    for n in range(first, loop_from):
        step(At(0, n, unroll))
    with eng.Fori(loop_from // unroll, loop_to // unroll) as j:
        for u in range(unroll):
            step(At(j, u, unroll))
    for n in range(loop_to, last):
        step(At(0, n, unroll))


def build(nc, x, src, dst, rel, w_rel, b_rel, w_ih, b_ih, b_hh, w1, b1, w2, b2, w3, b3, out):
    ctx = ExitStack()
    with ctx:
        ctx.enter_context(nc.allow_non_contiguous_dma(reason="bias columns, once"))

        def sb(name, shape, dt=F32):
            return ctx.enter_context(nc.sbuf_tensor(name, shape, dt))

        def sem(name):
            return ctx.enter_context(nc.semaphore(name))

        bank = [ctx.enter_context(nc.psum_tensor(f"bank{i}", [P, 512], F32)) for i in range(8)]

        agg = nc.dram_tensor("agg", (AGG_ROWS, D), F32).ap()
        dst_rows = nc.dram_tensor("dst_rows", (TILES, P), F32).ap()

        iota16 = sb("iota16", [P, P], F16)
        iotaf = sb("iotaf", [P, P])
        part_id = sb("part_id", [P, 1])
        ident = sb("ident", [P, P])
        ones = sb("ones", [P, P])
        ones16 = sb("ones16", [2, P], F16)
        earlier = sb("earlier", [P, 2, P])
        spare_row = sb("spare_row", [P, 2])
        pair_start = sb("pair_start", [1, BLOCKS, BLOCK_PAIRS])
        eps = sb("eps", [P, 1])

        src_slot = sb("src_slot", [P, TILES], I32)
        dst_slot = sb("dst_slot", [P, TILES])
        pair_rel = sb("pair_rel", [1, PAIRS], I32)

        REL_W = KH * 2 * D
        relT = sb("relT", [P, NUM_REL * REL_W], F16)
        relT_v = relT[:, :].rearrange("p (r k s o) -> p r k s o", r=NUM_REL, k=KH, s=2)
        ihT = sb("ihT", [P, KH, 2, CHUNKS * P], F32R)
        w1T = sb("w1T", [P, 2, KH * RH], F16)
        w2T = sb("w2T", [P, 2, RH], F16)
        w3T = sb("w3T", [P, 2, D], F16)
        brel_col = sb("brel_col", [P, NUM_REL * KH])
        brel_parts = sb("brel_parts", [2, NUM_REL * D], F16)
        bih_col = sb("bih_col", [P, 8])
        bhh_col = sb("bhh_col", [P, 8])
        gate_b = sb("gate_b", [P, 8])
        b1_col = sb("b1_col", [P, 1])
        b2_col = sb("b2_col", [P, 1])
        b3_all = sb("b3_all", [P, D])

        src_ring = sb("src_ring", [P, 4, 2], I32)
        dst_ring = sb("dst_ring", [P, 4, PAIR])
        xg = sb("xg", [P, 4, 2, D])
        stats = sb("stats", [P, 2, 2, 6])
        mean_var = sb("mean_var", [P, 4, 2, 2])
        std = sb("std", [P, 2, 2])
        rstd = sb("rstd", [P, 2, 2])
        xn = sb("xn", [P, 2, 2, D])
        s_hi = sb("s_hi", [P, 2, KH * PAIR], F16)
        s_lo = sb("s_lo", [P, 2, KH * PAIR], F16)
        h_f = sb("h_f", [P, 2, KH * PAIR])
        h_hi = sb("h_hi", [P, 2, KH * PAIR], F16)
        h_lo = sb("h_lo", [P, 2, KH * PAIR], F16)
        m_hi = sb("m_hi", [P, 2, 2 * D], F16)
        m_lo = sb("m_lo", [P, 2, 2 * D], F16)
        same_a = sb("same_a", [P, 2, P], F16)
        same_b = sb("same_b", [P, 2, PAIR], F16)
        before_tmp = sb("before_tmp", [P, 2, P + PAIR], F16)
        before = sb("before", [P, 4, 2])
        scatter_idx = sb("scatter_idx", [P, 4, 2], I32)
        summed = sb("summed", [P, 2, 2, D])

        prep_ctx = ExitStack()

        def tmp(name, shape, dt=F32):
            return prep_ctx.enter_context(nc.sbuf_tensor(name, shape, dt))

        upper = tmp("upper", [P, P])
        zeros = tmp("zeros", [P, ZERO_W])
        edge_i = tmp("edge_i", [ROWS, 3, BLOCKS, COLS], I32)
        rel_f = tmp("rel_f", [ROWS, BLOCKS, COLS])
        is_rel = tmp("is_rel", [ROWS, 2, BLOCKS, COLS])
        cum = tmp("cum", [ROWS, 2, BLOCKS, COLS])
        row_total = tmp("row_total", [ROWS, 2 * BLOCKS])
        prefix = tmp("prefix", [P, 4 * BLOCKS])
        slot_a = tmp("slot_a", [ROWS, BLOCKS, COLS])
        slot_b = tmp("slot_b", [ROWS, BLOCKS, COLS])
        slot_i = tmp("slot_i", [ROWS, BLOCKS, COLS], I32)
        tile_i = tmp("tile_i", [ROWS, BLOCKS, COLS], I32)
        tile_f = tmp("tile_f", [ROWS, BLOCKS * COLS])
        lane_f = tmp("lane_f", [ROWS, BLOCKS * COLS])
        pay_i = tmp("pay_i", [ROWS, NPAY, BLOCKS * COLS], I32)
        pay_f = tmp("pay_f", [ROWS, NPAY, BLOCKS * COLS])
        hot_lane = tmp("hot_lane", [ROWS, 4, P], F16)
        hot_tile = tmp("hot_tile", [ROWS, 4, NPAY, BLOCK_TILES], F16)
        dst_raw = tmp("dst_raw", [P, BLOCKS, BLOCK_TILES])
        dst_mark = tmp("dst_mark", [P, BLOCKS, BLOCK_TILES])
        dst_row_sb = tmp("dst_row_sb", [BLOCK_TILES, BLOCKS, P])
        rel_nat = tmp("rel_nat", [P, NUM_REL, KH, D])
        ih_nat = tmp("ih_nat", [P, CHUNKS, D])
        w1_nat = tmp("w1_nat", [P, D])
        w2_nat = tmp("w2_nat", [P, RH])
        w3_nat = tmp("w3_nat", [P, KH, RH])
        brel_row = tmp("brel_row", [2, NUM_REL * D])
        brel_hi = tmp("brel_hi", [2, NUM_REL * D], F16)
        prep_ctx.close()

        agg_in = sb("agg_in", [P, 2, UT, D])
        x_in = sb("x_in", [P, 2, UT, D])
        xb = sb("xb", [P, 2, UT, D])
        a_hi = sb("a_hi", [P, 2, KH, UNIT], F32R)
        a_lo = sb("a_lo", [P, 2, KH, UNIT], F32R)
        g_i = sb("g_i", [P, 2, UNIT])
        g_g = sb("g_g", [P, 2, UNIT])
        g_o = sb("g_o", [P, 2, UNIT])
        cell = sb("cell", [P, 2, UNIT])
        tcell = sb("tcell", [P, 2, UNIT])
        hn = sb("hn", [P, 2, UNIT])
        hn_hi = sb("hn_hi", [P, 2, KH, UNIT], F16)
        hn_lo = sb("hn_lo", [P, 2, KH, UNIT], F16)
        x1 = sb("x1", [P, UNIT])
        x1_hi = sb("x1_hi", [P, UNIT], F16)
        x1_lo = sb("x1_lo", [P, UNIT], F16)
        x2 = sb("x2", [P, UNIT])
        x2_hi = sb("x2_hi", [P, UNIT], F16)
        x2_lo = sb("x2_lo", [P, UNIT], F16)
        y = sb("y", [P, 2, UT, D])

        edges_in = sem("edges_in")
        weights_in = sem("weights_in")
        consts = sem("consts")
        zero_tile = sem("zero_tile")
        agg_zeroed = sem("agg_zeroed")
        prep = sem("prep")
        totals_ready = sem("totals_ready")
        prefix_ready = sem("prefix_ready")
        hot_ready = sem("hot_ready")
        hot_used = sem("hot_used")
        pair_rel_ready = sem("pair_rel_ready")
        src_slots_ready = sem("src_slots_ready")
        dst_slots_ready = sem("dst_slots_ready")
        dst_turned = sem("dst_turned")
        dst_row_ready = sem("dst_row_ready")
        dst_rows_stored = sem("dst_rows_stored")
        ident_ready = sem("ident_ready")
        w_turned = sem("w_turned")
        w_hi = sem("w_hi")
        w_lo = sem("w_lo")
        bias_ready = sem("bias_ready")

        src_loaded = [sem(f"src_loaded{i}") for i in range(4)]
        dst_loaded = [sem(f"dst_loaded{i}") for i in range(4)]
        gathered = [sem(f"gathered{i}") for i in range(4)]
        scattered = sem("scattered")
        gathers_cleared = sem("gathers_cleared")
        scatters_cleared = sem("scatters_cleared")
        stats_ready = sem("stats_ready")
        var_ready = sem("var_ready")
        std_ready = sem("std_ready")
        rstd_ready = sem("rstd_ready")
        normed = sem("normed")
        s_turned = sem("s_turned")
        s_hi_ready = sem("s_hi_ready")
        s_ready = sem("s_ready")
        h_done = sem("h_done")
        h_f_ready = sem("h_f_ready")
        h_hi_ready = sem("h_hi_ready")
        h_ready = sem("h_ready")
        m_done = sem("m_done")
        m_hi_ready = sem("m_hi_ready")
        m_ready = sem("m_ready")
        same_ready = sem("same_ready")
        before_ready = sem("before_ready")
        idx_ready = sem("idx_ready")
        sum_done = sem("sum_done")
        summed_ready = sem("summed_ready")

        agg_loaded = [sem(f"agg_loaded{i}") for i in range(2)]
        x_loaded = [sem(f"x_loaded{i}") for i in range(2)]
        stored = [sem(f"stored{i}") for i in range(2)]
        a_turned = sem("a_turned")
        a_hi_ready = sem("a_hi_ready")
        a_ready = sem("a_ready")
        chunk_done = sem("chunk_done")
        gate_ready = sem("gate_ready")
        cell_ready = sem("cell_ready")
        tcell_ready = sem("tcell_ready")
        hn_f_ready = sem("hn_f_ready")
        hn_hi_ready = sem("hn_hi_ready")
        hn_ready = sem("hn_ready")
        x1_done = sem("x1_done")
        x1_f_ready = sem("x1_f_ready")
        x1_hi_ready = sem("x1_hi_ready")
        x1_ready = sem("x1_ready")
        x2_done = sem("x2_done")
        x2_f_ready = sem("x2_f_ready")
        x2_hi_ready = sem("x2_hi_ready")
        x2_ready = sem("x2_ready")
        y_done = sem("y_done")
        xb_ready = sem("xb_ready")
        y_ready = sem("y_ready")

        def weight_groups():
            groups = []
            for r in range(NUM_REL):
                groups.append(([rel_nat[:, r, oc, k * P:(k + 1) * P] for k in range(KH) for oc in range(KH)],
                               [(0, KH * D, relT_v[:, r, :, 0, :], relT_v[:, r, :, 1, :], KH)]))
            half = CHUNKS // 2 * P
            for k in range(KH):
                for part in range(2):
                    cs = range(part * CHUNKS // 2, (part + 1) * CHUNKS // 2)
                    cols = slice(part * half, (part + 1) * half)
                    groups.append(([ih_nat[:, c, k * P:(k + 1) * P] for c in cs],
                                   [(0, half, ihT[:, k, 0, cols], ihT[:, k, 1, cols], 1)]))
            groups.append(([w1_nat[:, k * P:(k + 1) * P] for k in range(KH)] + [w2_nat[:, :]],
                           [(0, KH * RH, w1T[:, 0, :], w1T[:, 1, :], 1),
                            (KH * RH, KH * RH + RH, w2T[:, 0, :], w2T[:, 1, :], 1)]))
            groups.append(([w3_nat[:, oc, :] for oc in range(KH)], [(0, D, w3T[:, 0, :], w3T[:, 1, :], 1)]))
            return groups

        GROUPS = weight_groups()
        W_BANK = [bank[4 + g % 4] for g in range(len(GROUPS))]

        def part_view(b, lo, hi, k):
            v = b[:, lo:hi]
            return v.rearrange("p (k o) -> p k o", k=k) if k > 1 else v

        def plain(ap):
            return ap.bitcast(F32) if ap.dtype == F32R else ap

        B_T, B_H, B_M, B_G = (bank[0:2], bank[2:4], bank[4:6], bank[6:8])
        N_T, N_C, N_X, N_Y = (bank[0:2], bank[2:5], bank[5], bank[6:8])

        EDGE_RUN = dict(loop_from=8, loop_to=PAIRS - 8, unroll=4)
        NODE_RUN = dict(loop_from=4, loop_to=UNITS - 4, unroll=2)

        def unit_rows(u):
            return min(u * UNIT, NODES - UNIT) if isinstance(u, int) else u * UNIT

        def unit_view(t, u):
            return t[bass.ds(unit_rows(u), UNIT), :].rearrange("(p t) d -> p t d", t=UT)

        block = ctx.enter_context(nc.Block())

        @block.sync
        def _(sp):
            for i, t in enumerate((src, dst, rel)):
                sp.dma_start(edge_i[:, i, :, :], t.rearrange("(b p c) -> p b c", b=BLOCKS, c=COLS)).then_inc(edges_in, 16)
            for r in range(NUM_REL):
                sp.dma_start(rel_nat[:, r, :, :], w_rel[r, :, :].rearrange("(c p) i -> p c i", p=P)).then_inc(weights_in, 16)
            for c, row in enumerate(CHUNK_ROWS):
                sp.dma_start(ih_nat[:, c, :], w_ih[row:row + P, :]).then_inc(weights_in, 16)
            sp.dma_start(w1_nat[:, :], w1).then_inc(weights_in, 16)
            sp.dma_start(w2_nat[:, :], w2).then_inc(weights_in, 16)
            sp.dma_start(w3_nat[:, :, :], w3.rearrange("(c p) i -> p c i", p=P)).then_inc(weights_in, 16)
            sp.dma_start(brel_col[:, :], b_rel.rearrange("r (m p) -> p (r m)", p=P)).then_inc(weights_in, 16)
            sp.dma_start(brel_row[:, :], b_rel.rearrange("r d -> (r d)").partition_broadcast(2)).then_inc(weights_in, 16)
            sp.dma_start(bih_col[:, :], b_ih.rearrange("(c p) -> p c", p=P)).then_inc(weights_in, 16)
            sp.dma_start(bhh_col[:, :], b_hh.rearrange("(c p) -> p c", p=P)).then_inc(weights_in, 16)
            sp.dma_start(b1_col[:, :], b1.rearrange("(p c) -> p c", c=1)).then_inc(weights_in, 16)
            sp.dma_start(b2_col[:, :], b2.rearrange("(p c) -> p c", c=1)).then_inc(weights_in, 16)
            sp.dma_start(b3_all[:, :], b3.partition_broadcast(P)).then_inc(weights_in, 16)
            sp.wait_ge(dst_row_ready, 1)
            sp.dma_start(dst_rows.rearrange("(b t) p -> t b p", b=BLOCKS), dst_row_sb[:, :, :]).then_inc(dst_rows_stored, 16)
            sp.wait_ge(src_slots_ready, BLOCKS)
            sp.wait_ge(dst_rows_stored, 16)

            def step(at):
                k = at + 6
                if k.within(PAIRS):
                    wait_from(sp, gathered[k.slot(4)], k.turn(4) * 32)
                    sp.dma_start(src_ring[:, k.slot(4), :], src_slot[:, bass.ds(k.n * 2, 2)]).then_inc(src_loaded[k.slot(4)], 16)
                k = at
                if k.within(PAIRS):
                    wait_from(sp, before_ready, k.n - 3)
                    sp.dma_start(dst_ring[:, k.slot(4), :],
                                 dst_rows[bass.ds(k.n * 2, 2), :].rearrange("t p -> (t p)").partition_broadcast(P)
                                 ).then_inc(dst_loaded[k.slot(4)], 16)

            run_steps(sp, -6, last=PAIRS, step=step, **EDGE_RUN)

            sp.wait_ge(scattered, 32 * PAIRS)

            def node_step(at):
                k = at + 2
                if k.within(UNITS):
                    wait_from(sp, a_turned, k.n - 1)
                    sp.dma_start(agg_in[:, k.slot(2), :, :], unit_view(agg, k.n)).then_inc(agg_loaded[k.slot(2)], 16)
                k = at
                if k.within(UNITS):
                    wait_from(sp, xb_ready, k.n - 1)
                    sp.dma_start(x_in[:, k.slot(2), :, :], unit_view(x, k.n)).then_inc(x_loaded[k.slot(2)], 16)
                k = at - 3
                if k.within(UNITS):
                    sp.wait_ge(y_ready, k.n + 1)
                    if isinstance(k.n, int) and k.n == UNITS - 1:
                        sp.wait_ge(stored[(k - 1).slot(2)], 16 * ((k - 1).turn(2) + 1))
                    sp.dma_start(unit_view(out, k.n), y[:, k.slot(2), :, :]).then_inc(stored[k.slot(2)], 16)

            run_steps(sp, -2, last=UNITS + 3, step=node_step, **NODE_RUN)
            for s in range(2):
                sp.wait_ge(stored[s], 16 * len(range(s, UNITS, 2)))

        @block.gpsimd
        def _(pool):
            nc.gpsimd.iota(iota16[:, :], [[1, P]], base=0, channel_multiplier=0,
                           allow_small_or_imprecise_dtypes=True)
            nc.gpsimd.iota(iotaf[:, :], [[1, P]], base=0, channel_multiplier=0,
                           allow_small_or_imprecise_dtypes=True)
            nc.gpsimd.iota(part_id[:, :], [[1, 1]], base=0, channel_multiplier=1,
                           allow_small_or_imprecise_dtypes=True)
            nc.gpsimd.iota(spare_row[:, :], [[P, 2]], base=NODES, channel_multiplier=1,
                           allow_small_or_imprecise_dtypes=True)
            nc.gpsimd.iota(pair_start[:, :, :], [[0, BLOCKS], [PAIR, BLOCK_PAIRS]], base=0, channel_multiplier=0,
                           allow_small_or_imprecise_dtypes=True)
            nc.gpsimd.memset(ones[:, :], 1.0)
            nc.gpsimd.memset(ones16[:, :], 1.0)
            nc.gpsimd.memset(eps[:, :], LN_EPS).then_inc(consts, 1)

            def step(at):
                k = at - 4
                if k.within(PAIRS):
                    pool.wait_ge(idx_ready, k.n + 1)
                    pool.wait_ge(summed_ready, k.n + 1)
                    if isinstance(k.n, int) and k.n == 0:
                        pool.wait_ge(agg_zeroed, 16 * ZERO_DMAS)
                    wait_from(pool, scattered, k.n * 32)
                    pool.sem_inc(scatters_cleared, 1)
                    for t in range(2):
                        nc.gpsimd.indirect_dma_start(
                            out=agg[:, :],
                            out_offset=bass.IndirectOffsetOnAxis(ap=scatter_idx[:, k.slot(4), t:t + 1], axis=0),
                            in_=summed[:, k.slot(2), t, :], in_offset=None, compute_op=ALU.add).then_inc(scattered, 16)
                k = at + 4
                if k.within(PAIRS):
                    pool.wait_ge(src_loaded[k.slot(4)], 16 * (k.turn(4) + 1))
                    wait_from(pool, normed, k.n - 3)
                    pool.sem_inc(gathers_cleared, 1)
                    for t in range(2):
                        nc.gpsimd.indirect_dma_start(
                            out=xg[:, k.slot(4), t, :], out_offset=None, in_=x[:, :],
                            in_offset=bass.IndirectOffsetOnAxis(ap=src_ring[:, k.slot(4), t:t + 1], axis=0)
                        ).then_inc(gathered[k.slot(4)], 16)

            run_steps(pool, -4, last=PAIRS + 4, step=step, **EDGE_RUN)

            pool.wait_ge(weights_in, 16 * 18)

            def node_step(at):
                k = at - 1
                if k.within(UNITS):
                    pool.wait_ge(x_loaded[k.slot(2)], 16 * (k.turn(2) + 1))
                    wait_from(pool, y_ready, k.n - 1)
                    nc.gpsimd.tensor_tensor(xb[:, k.slot(2), :, :], x_in[:, k.slot(2), :, :],
                                            b3_all[:, :].unsqueeze(1).to_broadcast([P, UT, D]), ALU.add).then_inc(xb_ready, 1)

            run_steps(pool, 1, last=UNITS + 1, step=node_step, **NODE_RUN)

        @block.scalar
        def _(act):
            act.wait_ge(zero_tile, 1)
            agg_z = agg.rearrange("(p r) d -> p (r d)", p=P).rearrange("p (n w) -> p n w", w=ZERO_W)
            per = ZERO_REPS // ZERO_DMAS
            for i in range(ZERO_DMAS):
                act.dma_start(agg_z[:, i * per:(i + 1) * per, :],
                              zeros[:, :].unsqueeze(1).to_broadcast([P, per, ZERO_W])).then_inc(agg_zeroed, 16)
            for g, (_, targets) in enumerate(GROUPS):
                act.wait_ge(w_turned, g + 1)
                for lo, hi, to_hi, _, k in targets:
                    last = nc.scalar.copy(to_hi, part_view(W_BANK[g], lo, hi, k))
                last.then_inc(w_hi, 1)
            act.wait_ge(consts, 1)
            act.wait_ge(pair_rel_ready, 1)
            act.wait_ge(weights_in, 16 * 18)

            def step(at):
                k = at + 1
                if k.within(PAIRS):
                    act.wait_ge(var_ready, k.n + 1)
                    nc.scalar.activation(std[:, k.slot(2), :], mean_var[:, k.slot(4), :, 1], ACT.Sqrt,
                                         bias=eps[:, 0:1]).then_inc(std_ready, 1)
                k = at
                if k.within(PAIRS):
                    act.wait_ge(s_turned, k.n + 1)
                    nc.scalar.activation(s_hi[:, k.slot(2), :], B_T[k.slot(2)][:, :], ACT.Relu).then_inc(s_hi_ready, 1)
                k = at - 1
                if k.within(PAIRS):
                    r = act.value_load(pair_rel[0:1, bass.ds(k.n, 1)], min_val=0, max_val=1)
                    act.wait_ge(h_done, k.n + 1)
                    for m in range(KH):
                        last = nc.scalar.activation(h_f[:, k.slot(2), m * PAIR:(m + 1) * PAIR],
                                                    B_H[k.slot(2)][:, m * PAIR:(m + 1) * PAIR], ACT.Relu,
                                                    bias=brel_col[:, bass.ds(r * KH + m, 1)])
                    last.then_inc(h_f_ready, 1)
                k = at - 2
                if k.within(PAIRS):
                    act.wait_ge(m_done, k.n + 1)
                    nc.scalar.activation(m_hi[:, k.slot(2), :], B_M[k.slot(2)][:, :], ACT.Relu).then_inc(m_hi_ready, 1)
                k = at - 1
                if k.within(PAIRS):
                    act.wait_ge(h_f_ready, k.n + 1)
                    nc.scalar.copy(h_hi[:, k.slot(2), :], h_f[:, k.slot(2), :]).then_inc(h_hi_ready, 1)
                k = at - 3
                if k.within(PAIRS):
                    act.wait_ge(sum_done, k.n + 1)
                    wait_from(act, scattered, (k.n - 1) * 32)
                    nc.scalar.copy(summed[:, k.slot(2), :, :].rearrange("p t d -> p (t d)"),
                                   B_G[k.slot(2)][:, :]).then_inc(summed_ready, 1)

            run_steps(act, -1, last=PAIRS + 3, step=step, **EDGE_RUN)

            def gate(k, c):
                half = c // 3
                to, fn = ((g_i, ACT.Sigmoid), (g_g, ACT.Tanh), (g_o, ACT.Sigmoid))[c % 3]
                act.wait_ge(chunk_done, k.n * CHUNKS + c + 1)
                col = CHUNK_ROWS[c] // P
                nc.scalar.activation(to[:, half, :], N_C[c % 3][:, :], fn,
                                     bias=gate_b[:, col:col + 1]).then_inc(gate_ready, 1)

            def tanh_cell(k, half):
                act.wait_ge(cell_ready, k.n * KH + half + 1)
                nc.scalar.activation(tcell[:, half, :], cell[:, half, :], ACT.Tanh).then_inc(tcell_ready, 1)

            def node_step(at):
                if at.within(UNITS):
                    for c in range(3):
                        gate(at, c)
                    tanh_cell(at, 0)
                k = at - 1
                if k.within(UNITS):
                    act.wait_ge(x1_done, k.n + 1)
                    nc.scalar.activation(x1[:, :], N_X[:, :], ACT.Relu, bias=b1_col[:, 0:1]).then_inc(x1_f_ready, 1)
                if at.within(UNITS):
                    gate(at, 3)
                k = at + 1
                if k.within(UNITS):
                    act.wait_ge(a_turned, k.n + 1)
                    for h in range(KH):
                        nc.scalar.copy(a_hi[:, k.slot(2), h, :], N_T[h][:, :]).then_inc(a_hi_ready, 1)
                if at.within(UNITS):
                    gate(at, 4)
                k = at - 1
                if k.within(UNITS):
                    act.wait_ge(x2_done, k.n + 1)
                    nc.scalar.activation(x2[:, :], N_X[:, :], ACT.Relu, bias=b2_col[:, 0:1]).then_inc(x2_f_ready, 1)
                if at.within(UNITS):
                    gate(at, 5)
                    tanh_cell(at, 1)

            run_steps(act, -1, last=UNITS + 1, step=node_step, **NODE_RUN)

        @block.vector
        def _(dve):
            done = [0]

            def chained(ins):
                done[0] += 1
                ins.then_inc(prep, 1)
                dve.wait_ge(prep, done[0])

            nc.vector.memset(zeros[:, :], 0.0).then_inc(zero_tile, 1)
            dve.wait_ge(consts, 1)
            nc.vector.tensor_scalar(ident[:, :], iotaf[:, :], part_id[:, 0:1], None, ALU.is_equal)
            nc.vector.tensor_scalar(upper[:, :], iotaf[:, :], part_id[:, 0:1], None, ALU.is_gt).then_inc(ident_ready, 1)
            nc.vector.memset(earlier[:, 0, :], SPARE)
            nc.vector.tensor_scalar(earlier[:, 1, :], iotaf[:, :], part_id[:, 0:1], SPARE, ALU.is_lt, ALU.mult)

            dve.wait_ge(edges_in, 48)
            chained(nc.vector.tensor_copy(rel_f[:, :, :], edge_i[:, 2, :, :]))
            for r in range(NUM_REL):
                last = nc.vector.tensor_scalar(is_rel[:, r, :, :], rel_f[:, :, :], float(r), None, ALU.is_equal)
            chained(last)
            for r in range(NUM_REL):
                for b in range(BLOCKS):
                    last = nc.vector.tensor_tensor_scan(cum[:, r, b, :], is_rel[:, r, b, :], zeros[0:ROWS, 0:COLS], 0.0,
                                                        ALU.add, ALU.add)
            chained(last)
            nc.vector.tensor_copy(row_total[:, :].rearrange("p (r b) -> p r b", r=2), cum[:, :, :, COLS - 1]).then_inc(totals_ready, 1)
            nc.vector.tensor_scalar(pay_i[:, 0, :], edge_i[:, 0, :, :].rearrange("p b c -> p (b c)"), 8, None,
                                    ALU.arith_shift_right)
            nc.vector.tensor_scalar(pay_i[:, 1, :], edge_i[:, 0, :, :].rearrange("p b c -> p (b c)"), 255, None,
                                    ALU.bitwise_and)
            chained(nc.vector.tensor_scalar(tile_i[:, :, :], edge_i[:, 1, :, :], 1.0, None, ALU.add))
            nc.vector.tensor_scalar(pay_i[:, 2, :], tile_i[:, :, :].rearrange("p b c -> p (b c)"), 8, None,
                                    ALU.arith_shift_right)
            chained(nc.vector.tensor_scalar(pay_i[:, 3, :], tile_i[:, :, :].rearrange("p b c -> p (b c)"), 255, None,
                                            ALU.bitwise_and))
            nc.vector.tensor_copy(pay_f[:, :, :], pay_i[:, :, :])
            dve.wait_ge(prefix_ready, 1)
            chained(nc.vector.tensor_copy(prefix[:, :], bank[0][:, 0:4 * BLOCKS]))
            nc.vector.tensor_tensor(pair_rel[:, :].rearrange("p (b q) -> p b q", b=BLOCKS), pair_start[:, :, :],
                                    prefix[0:1, 2 * BLOCKS:3 * BLOCKS].unsqueeze(2).to_broadcast([1, BLOCKS, BLOCK_PAIRS]),
                                    ALU.is_ge).then_inc(pair_rel_ready, 1)
            for b in range(BLOCKS):
                nc.vector.tensor_scalar(slot_a[:, b, :], cum[:, 0, b, :], prefix[0:ROWS, b:b + 1],
                                        -1.0 - BLOCK_SLOTS, ALU.add, ALU.add)
                last = nc.vector.tensor_scalar(slot_b[:, b, :], cum[:, 1, b, :], prefix[0:ROWS, BLOCKS + b:BLOCKS + b + 1],
                                               -1.0, ALU.add, ALU.mult)
            chained(last)
            nc.vector.tensor_tensor(slot_a[:, :, :], slot_a[:, :, :], is_rel[:, 0, :, :], ALU.mult)
            chained(nc.vector.tensor_tensor(slot_b[:, :, :], slot_b[:, :, :], is_rel[:, 1, :, :], ALU.mult))
            chained(nc.vector.scalar_tensor_tensor(out=slot_i[:, :, :].rearrange("p b c -> p (b c)"),
                                                   in0=slot_a[:, :, :].rearrange("p b c -> p (b c)"),
                                                   scalar=float(BLOCK_SLOTS),
                                                   in1=slot_b[:, :, :].rearrange("p b c -> p (b c)"),
                                                   op0=ALU.add, op1=ALU.add))
            chained(nc.vector.tensor_scalar(tile_i[:, :, :], slot_i[:, :, :], 7, None, ALU.arith_shift_right))
            chained(nc.vector.tensor_copy(tile_f[:, :], tile_i[:, :, :].rearrange("p b c -> p (b c)")))
            chained(nc.vector.tensor_scalar(tile_i[:, :, :], slot_i[:, :, :], P - 1, None, ALU.bitwise_and))
            chained(nc.vector.tensor_copy(lane_f[:, :], tile_i[:, :, :].rearrange("p b c -> p (b c)")))

            for g, (_, targets) in enumerate(GROUPS):
                dve.wait_ge(w_hi, g + 1)
                for lo, hi, to_hi, to_lo, k in targets:
                    last = nc.vector.tensor_tensor(to_lo, part_view(W_BANK[g], lo, hi, k), plain(to_hi), ALU.subtract)
                last.then_inc(w_lo, 1)
            dve.wait_ge(weights_in, 16 * 18)
            nc.vector.tensor_tensor(gate_b[:, :], bih_col[:, :], bhh_col[:, :], ALU.add)
            chained(nc.vector.tensor_copy(brel_hi[:, :], brel_row[:, :]))
            chained(nc.vector.tensor_tensor(brel_parts[:, :], brel_row[:, :], brel_hi[:, :], ALU.subtract))
            nc.vector.tensor_copy(brel_parts[0:1, :], brel_hi[0:1, :]).then_inc(bias_ready, 1)

            def hot_column(b, j, q):
                col = b * COLS + j
                wait_from(dve, hot_used, col - 3)
                nc.vector.tensor_scalar(hot_lane[:, q, :], iota16[0:ROWS, :], lane_f[:, bass.ds(col, 1)], None, ALU.is_equal)
                for n in range(NPAY):
                    last = nc.vector.tensor_scalar(hot_tile[:, q, n, :], iota16[0:ROWS, 0:BLOCK_TILES],
                                                   tile_f[:, bass.ds(col, 1)], pay_f[:, n, bass.ds(col, 1)],
                                                   ALU.is_equal, ALU.mult)
                last.then_inc(hot_ready, 1)

            for b in range(BLOCKS):
                for j in range(4):
                    hot_column(b, j, j)
                with dve.Fori(1, COLS // 4 - 1) as g:
                    for q in range(4):
                        hot_column(b, g * 4 + q, q)
                for j in range(COLS - 4, COLS):
                    hot_column(b, j, j % 4)
                dve.wait_ge(hot_used, (b + 1) * COLS)
                cols = slice(b * BLOCK_TILES, (b + 1) * BLOCK_TILES)
                byte = [bank[b][:, n * BLOCK_TILES:(n + 1) * BLOCK_TILES] for n in range(NPAY)]
                nc.vector.tensor_copy(dst_mark[:, b, :], byte[1])
                chained(nc.vector.tensor_copy(dst_raw[:, b, :], byte[3]))
                nc.vector.scalar_tensor_tensor(out=src_slot[:, cols], in0=byte[0], scalar=256.0, in1=dst_mark[:, b, :],
                                               op0=ALU.mult, op1=ALU.add).then_inc(src_slots_ready, 1)
                chained(nc.vector.scalar_tensor_tensor(out=dst_raw[:, b, :], in0=byte[2], scalar=256.0,
                                                       in1=dst_raw[:, b, :], op0=ALU.mult, op1=ALU.add))
                chained(nc.vector.tensor_scalar(dst_mark[:, b, :], dst_raw[:, b, :], 0.0, FAR, ALU.is_equal, ALU.mult))
                nc.vector.scalar_tensor_tensor(out=dst_slot[:, cols], in0=dst_raw[:, b, :], scalar=-1.0,
                                               in1=dst_mark[:, b, :], op0=ALU.add, op1=ALU.add).then_inc(dst_slots_ready, 1)
            dve.wait_ge(dst_turned, 1)
            for b in range(BLOCKS):
                last = nc.vector.tensor_copy(dst_row_sb[:, b, :], bank[4][0:BLOCK_TILES, b * P:(b + 1) * P])
            last.then_inc(dst_row_ready, 1)
            dve.wait_ge(dst_slots_ready, BLOCKS)

            def step(at):
                k = at + 2
                if k.within(PAIRS):
                    dve.wait_ge(gathered[k.slot(4)], 32 * (k.turn(4) + 1))
                    for t in range(2):
                        last = nc.vector.bn_stats(stats[:, k.slot(2), t, :], xg[:, k.slot(4), t, :])
                    last.then_inc(stats_ready, 1)
                k = at
                if k.within(PAIRS):
                    dve.wait_ge(s_hi_ready, k.n + 1)
                    nc.vector.scalar_tensor_tensor(out=s_lo[:, k.slot(2), :], in0=B_T[k.slot(2)][:, :], scalar=0.0,
                                                   in1=s_hi[:, k.slot(2), :], op0=ALU.max,
                                                   op1=ALU.subtract).then_inc(s_ready, 1)
                k = at + 1
                if k.within(PAIRS):
                    dve.wait_ge(std_ready, k.n + 1)
                    if (k + 1).within(PAIRS):
                        dve.wait_ge(stats_ready, k.n + 2)
                    nc.vector.reciprocal(rstd[:, k.slot(2), :], std[:, k.slot(2), :]).then_inc(rstd_ready, 1)
                k = at + 2
                if k.within(PAIRS):
                    if isinstance(k.n, int) and k.n == 0:
                        dve.wait_ge(stats_ready, 1)
                    for t in range(2):
                        last = nc.vector.bn_aggr(mean_var[:, k.slot(4), t, :], stats[:, k.slot(2), t, :])
                    last.then_inc(var_ready, 1)
                k = at + 1
                if k.within(PAIRS):
                    dve.wait_ge(rstd_ready, k.n + 1)
                    for t in range(2):
                        last = nc.vector.tensor_scalar(xn[:, k.slot(2), t, :], xg[:, k.slot(4), t, :],
                                                       mean_var[:, k.slot(4), t, 0:1], rstd[:, k.slot(2), t:t + 1],
                                                       ALU.subtract, ALU.mult)
                    last.then_inc(normed, 1)
                k = at - 2
                if k.within(PAIRS):
                    dve.wait_ge(dst_loaded[k.slot(4)], 16 * (k.turn(4) + 1))
                    if not at.within(PAIRS):
                        dve.wait_ge(sum_done, k.n - 1)
                    nc.vector.tensor_scalar(same_a[:, k.slot(2), :], dst_ring[:, k.slot(4), 0:P],
                                            dst_slot[:, bass.ds(k.n * 2, 1)], None, ALU.is_equal)
                    nc.vector.tensor_scalar(same_b[:, k.slot(2), :], dst_ring[:, k.slot(4), :],
                                            dst_slot[:, bass.ds(k.n * 2 + 1, 1)], None, ALU.is_equal).then_inc(same_ready, 1)
                    dve.wait_ge(m_hi_ready, k.n + 1)
                    nc.vector.scalar_tensor_tensor(out=m_lo[:, k.slot(2), :], in0=B_M[k.slot(2)][:, :], scalar=0.0,
                                                   in1=m_hi[:, k.slot(2), :], op0=ALU.max,
                                                   op1=ALU.subtract).then_inc(m_ready, 1)
                k = at - 1
                if k.within(PAIRS):
                    dve.wait_ge(h_hi_ready, k.n + 1)
                    nc.vector.tensor_tensor(h_lo[:, k.slot(2), :], h_f[:, k.slot(2), :], h_hi[:, k.slot(2), :],
                                            ALU.subtract).then_inc(h_ready, 1)
                k = at - 2
                if k.within(PAIRS):
                    nc.vector.scalar_tensor_tensor(out=before_tmp[:, k.slot(2), 0:P], in0=dst_ring[:, k.slot(4), 0:P],
                                                   scalar=dst_slot[:, bass.ds(k.n * 2, 1)], in1=earlier[:, 1, :],
                                                   op0=ALU.is_equal, op1=ALU.mult, accum_out=before[:, k.slot(4), 0:1])
                    nc.vector.scalar_tensor_tensor(out=before_tmp[:, k.slot(2), P:P + PAIR], in0=dst_ring[:, k.slot(4), :],
                                                   scalar=dst_slot[:, bass.ds(k.n * 2 + 1, 1)],
                                                   in1=earlier[:, :, :].rearrange("p a b -> p (a b)"),
                                                   op0=ALU.is_equal, op1=ALU.mult,
                                                   accum_out=before[:, k.slot(4), 1:2]).then_inc(before_ready, 1)
                k = at - 3
                if k.within(PAIRS):
                    dve.wait_ge(before_ready, k.n + 1)
                    for t in range(2):
                        last = nc.vector.tensor_scalar(scatter_idx[:, k.slot(4), t:t + 1], before[:, k.slot(4), t:t + 1],
                                                       dst_slot[:, bass.ds(k.n * 2 + t, 1)], spare_row[:, t:t + 1],
                                                       ALU.add, ALU.min)
                    last.then_inc(idx_ready, 1)

            run_steps(dve, -2, last=PAIRS + 3, step=step, **EDGE_RUN)

            def cell_of(k, half):
                dve.wait_ge(gate_ready, k.n * CHUNKS + half * 3 + 2)
                nc.vector.tensor_tensor(cell[:, half, :], g_i[:, half, :], g_g[:, half, :], ALU.mult).then_inc(cell_ready, 1)

            def hidden(k, half):
                dve.wait_ge(tcell_ready, k.n * KH + half + 1)
                nc.vector.tensor_tensor(hn[:, half, :], g_o[:, half, :], tcell[:, half, :], ALU.mult).then_inc(hn_f_ready, 1)

            def hidden_hi(k, half):
                dve.wait_ge(hn_f_ready, k.n * KH + half + 1)
                nc.vector.tensor_copy(hn_hi[:, k.slot(2), half, :], hn[:, half, :]).then_inc(hn_hi_ready, 1)

            def hidden_lo(k, half):
                dve.wait_ge(hn_hi_ready, k.n * KH + half + 1)
                nc.vector.tensor_tensor(hn_lo[:, k.slot(2), half, :], hn[:, half, :], hn_hi[:, k.slot(2), half, :],
                                        ALU.subtract).then_inc(hn_ready, 1)

            def result(k, part):
                rows = slice(part * UT // 2, (part + 1) * UT // 2)
                if part == 0:
                    dve.wait_ge(y_done, k.n + 1)
                    dve.wait_ge(xb_ready, k.n + 1)
                    wait_from(dve, stored[k.slot(2)], 16 * k.turn(2))
                ins = nc.vector.tensor_tensor(y[:, k.slot(2), rows, :].rearrange("p t d -> p (t d)"), N_Y[part][:, :],
                                              xb[:, k.slot(2), rows, :].rearrange("p t d -> p (t d)"), ALU.add)
                if part == 1:
                    ins.then_inc(y_ready, 1)

            def node_step(at):
                if at.within(UNITS):
                    cell_of(at, 0)
                if (at - 2).within(UNITS):
                    result(at - 2, 0)
                if at.within(UNITS):
                    hidden(at, 0)
                if (at - 2).within(UNITS):
                    result(at - 2, 1)
                if at.within(UNITS):
                    hidden_hi(at, 0)
                k = at - 1
                if k.within(UNITS):
                    dve.wait_ge(x1_f_ready, k.n + 1)
                    nc.vector.tensor_copy(x1_hi[:, :], x1[:, :]).then_inc(x1_hi_ready, 1)
                if at.within(UNITS):
                    hidden_lo(at, 0)
                if k.within(UNITS):
                    dve.wait_ge(x1_hi_ready, k.n + 1)
                    nc.vector.tensor_tensor(x1_lo[:, :], x1[:, :], x1_hi[:, :], ALU.subtract).then_inc(x1_ready, 1)
                k = at + 1
                if k.within(UNITS):
                    for h in range(KH):
                        dve.wait_ge(a_hi_ready, k.n * KH + h + 1)
                        last = nc.vector.tensor_tensor(a_lo[:, k.slot(2), h, :], N_T[h][:, :],
                                                       plain(a_hi[:, k.slot(2), h, :]), ALU.subtract)
                    last.then_inc(a_ready, 1)
                if at.within(UNITS):
                    cell_of(at, 1)
                k = at - 1
                if k.within(UNITS):
                    dve.wait_ge(x2_f_ready, k.n + 1)
                    nc.vector.tensor_copy(x2_hi[:, :], x2[:, :]).then_inc(x2_hi_ready, 1)
                if at.within(UNITS):
                    hidden(at, 1)
                if k.within(UNITS):
                    dve.wait_ge(x2_hi_ready, k.n + 1)
                    nc.vector.tensor_tensor(x2_lo[:, :], x2[:, :], x2_hi[:, :], ALU.subtract).then_inc(x2_ready, 1)
                if at.within(UNITS):
                    hidden_hi(at, 1)
                    hidden_lo(at, 1)

            run_steps(dve, -1, last=UNITS + 2, step=node_step, **NODE_RUN)

        @block.tensor
        def _(pe):
            pe.wait_ge(ident_ready, 1)
            pe.wait_ge(totals_ready, 1)
            nc.tensor.matmul(bank[0][:, 0:2 * BLOCKS], upper[0:ROWS, :], row_total[:, :], start=True, stop=True)
            nc.tensor.matmul(bank[0][:, 2 * BLOCKS:4 * BLOCKS], ones[0:ROWS, :], row_total[:, :],
                             start=True, stop=True).then_inc(prefix_ready, 1)
            pe.wait_ge(weights_in, 16 * 18)
            for g, (blocks, _) in enumerate(GROUPS):
                wait_from(pe, w_lo, g - 3)
                for i, w in enumerate(blocks):
                    last = nc.tensor.transpose(W_BANK[g][:, i * P:(i + 1) * P], w, ident[:, :])
                last.then_inc(w_turned, 1)
            def place_column(b, j, q, start, stop):
                pe.wait_ge(hot_ready, b * COLS + j + 1)
                nc.tensor.matmul(bank[b][:, 0:NPAY * BLOCK_TILES], hot_lane[:, q, :],
                                 hot_tile[:, q, :, :].rearrange("p n t -> p (n t)"),
                                 start=start, stop=stop).then_inc(hot_used, 1)

            for b in range(BLOCKS):
                for j in range(4):
                    place_column(b, j, j, j == 0, False)
                with pe.Fori(1, COLS // 4 - 1) as g:
                    for q in range(4):
                        place_column(b, g * 4 + q, q, False, False)
                for j in range(COLS - 4, COLS):
                    place_column(b, j, j % 4, False, j == COLS - 1)
            pe.wait_ge(w_lo, len(GROUPS))
            pe.wait_ge(dst_slots_ready, BLOCKS)
            for b in range(BLOCKS):
                last = nc.tensor.transpose(bank[4][0:BLOCK_TILES, b * P:(b + 1) * P],
                                           dst_slot[:, b * BLOCK_TILES:(b + 1) * BLOCK_TILES], ident[:, :])
            last.then_inc(dst_turned, 1)
            pe.wait_ge(bias_ready, 1)
            pe.wait_ge(pair_rel_ready, 1)
            pe.wait_ge(dst_row_ready, 1)

            def products(parts):
                (a_h, a_l), (b_h, b_l) = parts
                return (a_h, b_h), (a_l, b_h), (a_h, b_l)

            def step(at):
                k = at
                if k.within(PAIRS):
                    pe.wait_ge(normed, k.n + 1)
                    for h in range(KH):
                        for t in range(2):
                            c = h * PAIR + t * P
                            last = nc.tensor.transpose(B_T[k.slot(2)][:, c:c + P],
                                                       xn[:, k.slot(2), t, h * P:(h + 1) * P], ident[:, :])
                    last.then_inc(s_turned, 1)
                k = at - 1
                if k.within(PAIRS):
                    r = pe.value_load(pair_rel[0:1, bass.ds(k.n, 1)], min_val=0, max_val=1)
                    pe.wait_ge(s_ready, k.n + 1)
                    for m in range(KH):
                        ps = B_H[k.slot(2)][:, m * PAIR:(m + 1) * PAIR]
                        todo = []
                        for kk in range(KH):
                            w = [relT[:, bass.ds(r * REL_W + (kk * 2 + s) * D + m * P, P)] for s in range(2)]
                            v = [t[:, k.slot(2), kk * PAIR:(kk + 1) * PAIR] for t in (s_hi, s_lo)]
                            todo += products((w, v))
                        for i, (lhs, rhs) in enumerate(todo):
                            last = nc.tensor.matmul(ps, lhs, rhs, start=i == 0, stop=i == len(todo) - 1)
                    last.then_inc(h_done, 1)
                k = at - 2
                if k.within(PAIRS):
                    r = pe.value_load(pair_rel[0:1, bass.ds(k.n, 1)], min_val=0, max_val=1)
                    pe.wait_ge(h_ready, k.n + 1)
                    for t in range(2):
                        ps = B_M[k.slot(2)][:, t * D:(t + 1) * D]
                        nc.tensor.matmul(ps, ones16[:, :], brel_parts[:, bass.ds(r * D, D)], start=True, stop=False)
                        todo = []
                        for kk in range(KH):
                            c = kk * PAIR + t * P
                            w = [relT[:, bass.ds(r * REL_W + (kk * 2 + s) * D, D)] for s in range(2)]
                            v = [u[:, k.slot(2), c:c + P] for u in (h_hi, h_lo)]
                            todo += products((v, w))
                        for i, (lhs, rhs) in enumerate(todo):
                            last = nc.tensor.matmul(ps, lhs, rhs, start=False, stop=i == len(todo) - 1)
                    last.then_inc(m_done, 1)
                k = at - 3
                if k.within(PAIRS):
                    pe.wait_ge(m_ready, k.n + 1)
                    pe.wait_ge(same_ready, k.n + 1)
                    wait_from(pe, summed_ready, k.n - 1)
                    s = k.slot(2)
                    for ps, todo in (
                        (B_G[s][:, 0:D], [(same_a[:, s, :], m[:, s, 0:D]) for m in (m_hi, m_lo)]
                         + [(same_b[:, s, 0:P], m[:, s, D:2 * D]) for m in (m_hi, m_lo)]),
                        (B_G[s][:, D:2 * D], [(same_b[:, s, P:PAIR], m[:, s, D:2 * D]) for m in (m_hi, m_lo)]),
                    ):
                        for i, (lhs, rhs) in enumerate(todo):
                            last = nc.tensor.matmul(ps, lhs, rhs, start=i == 0, stop=i == len(todo) - 1)
                    last.then_inc(sum_done, 1)

            run_steps(pe, 0, last=PAIRS + 3, step=step, **EDGE_RUN)

            pe.wait_ge(summed_ready, PAIRS)

            def chunk(k, c):
                wait_from(pe, gate_ready, k.n * CHUNKS + c - 2)
                if c == 0:
                    pe.wait_ge(a_ready, k.n + 1)
                todo = []
                for kk in range(KH):
                    w = [ihT[:, kk, s, c * P:(c + 1) * P] for s in range(2)]
                    v = [t[:, k.slot(2), kk, :] for t in (a_hi, a_lo)]
                    todo += products((w, v))
                for i, (lhs, rhs) in enumerate(todo):
                    last = nc.tensor.matmul(N_C[c % 3][:, :], lhs, rhs, start=i == 0, stop=i == len(todo) - 1)
                last.then_inc(chunk_done, 1)

            def turn_agg(k):
                pe.wait_ge(agg_loaded[k.slot(2)], 16 * (k.turn(2) + 1))
                wait_from(pe, a_ready, k.n)
                for h in range(KH):
                    for t in range(UT):
                        last = nc.tensor.transpose(N_T[h][:, t * P:(t + 1) * P],
                                                   agg_in[:, k.slot(2), t, h * P:(h + 1) * P], ident[:, :])
                last.then_inc(a_turned, 1)

            def mlp1(k):
                pe.wait_ge(hn_ready, (k.n + 1) * KH)
                wait_from(pe, x2_f_ready, k.n)
                todo = []
                for kk in range(KH):
                    w = [w1T[:, s, kk * RH:(kk + 1) * RH] for s in range(2)]
                    v = [t[:, k.slot(2), kk, :] for t in (hn_hi, hn_lo)]
                    todo += products((w, v))
                for i, (lhs, rhs) in enumerate(todo):
                    last = nc.tensor.matmul(N_X[:, :], lhs, rhs, start=i == 0, stop=i == len(todo) - 1)
                last.then_inc(x1_done, 1)

            def mlp2(k):
                pe.wait_ge(x1_ready, k.n + 1)
                todo = products(([w2T[:, s, :] for s in range(2)], (x1_hi[:, :], x1_lo[:, :])))
                for i, (lhs, rhs) in enumerate(todo):
                    last = nc.tensor.matmul(N_X[:, :], lhs, rhs, start=i == 0, stop=i == len(todo) - 1)
                last.then_inc(x2_done, 1)

            def mlp3(k):
                pe.wait_ge(x2_ready, k.n + 1)
                wait_from(pe, y_ready, k.n)
                for t in range(UT):
                    v = [u[:, t * P:(t + 1) * P] for u in (x2_hi, x2_lo)]
                    todo = products((v, [w3T[:, s, :] for s in range(2)]))
                    for i, (lhs, rhs) in enumerate(todo):
                        last = nc.tensor.matmul(N_Y[t // 2][:, (t % 2) * D:(t % 2 + 1) * D], lhs, rhs,
                                                start=i == 0, stop=i == len(todo) - 1)
                last.then_inc(y_done, 1)

            def node_step(at):
                now, last, older, after = (at.within(UNITS), (at - 1).within(UNITS), (at - 2).within(UNITS),
                                           (at + 1).within(UNITS))
                if now:
                    chunk(at, 0)
                    chunk(at, 1)
                if older:
                    mlp3(at - 2)
                if now:
                    chunk(at, 2)
                if last:
                    mlp1(at - 1)
                if now:
                    chunk(at, 3)
                if after:
                    turn_agg(at + 1)
                if now:
                    chunk(at, 4)
                if last:
                    mlp2(at - 1)
                if now:
                    chunk(at, 5)

            run_steps(pe, -1, last=UNITS + 2, step=node_step, **NODE_RUN)


_INS = ['x', 'src', 'dst', 'edge_type_2', 'L0_gnn_W_rel', 'L0_gnn_b_rel', 'L0_gnn_W_ih', 'L0_gnn_b_ih',
        'L0_gnn_b_hh', 'L0_gnn_W1', 'L0_gnn_b1', 'L0_gnn_W2', 'L0_gnn_b2', 'L0_gnn_W3', 'L0_gnn_b3']


def kernel(**inputs):
    import numpy as _np
    import concourse.bacc as _bacc
    from concourse import mybir as _mybir
    from concourse.bass_utils import run_bass_kernel_spmd as _run

    nc = _bacc.Bacc("TRN2", target_bir_lowering=False, num_devices=1)
    arrays, args = {}, []
    for name in _INS:
        a = _np.ascontiguousarray(inputs[name])
        arrays[f"in_{name}"] = a
        args.append(nc.dram_tensor(f"in_{name}", a.shape, _mybir.dt.from_np(a.dtype), kind="ExternalInput").ap())
    args.append(nc.dram_tensor("out_0", (NODES, D), _mybir.dt.float32, kind="ExternalOutput").ap())
    build(nc, *args)
    r = _run(nc, [arrays], core_ids=[0])
    return r.results[0]["out_0"]
```

```python
import concourse.bass as bass
from concourse import mybir
from contextlib import ExitStack

F32 = mybir.dt.float32
F32R = mybir.dt.float32r
F16 = mybir.dt.float16
I32 = mybir.dt.int32
ALU = mybir.AluOpType
ACT = mybir.ActivationFunctionType

P = 128
D = 256
KH = D // P
NODES = 50000
EDGES = 50000
NUM_REL = 2
LN_EPS = 1e-5

BLOCKS = 4
ROWS = 125
COLS = EDGES // BLOCKS // ROWS
PAIR = 2 * P
BLOCK_PAIRS = (ROWS * COLS + 2 * (PAIR - 1)) // PAIR
BLOCK_TILES = 2 * BLOCK_PAIRS
BLOCK_SLOTS = BLOCK_PAIRS * PAIR
PAIRS = BLOCKS * BLOCK_PAIRS
TILES = 2 * PAIRS
PARTS = 3
SRC_LOW, DST_LOW = 5, 10
DST_HIGH = NODES.bit_length() - DST_LOW
assert max(NODES.bit_length() - SRC_LOW, SRC_LOW + DST_HIGH, DST_LOW) <= 11
BATCH = 10
BATCHES = COLS // BATCH

SPARE = 65536.0
FAR = 1.0e6

AGG_ROWS = -(-(NODES + PAIR) // P) * P
AGG_PART = AGG_ROWS // P * D
ZERO_REPS = 48
ZERO_W = AGG_PART // ZERO_REPS
assert ZERO_W * ZERO_REPS == AGG_PART
ZERO_DMAS = 6

UNIT = 512
UT = UNIT // P
UNITS = -(-NODES // UNIT)
CHUNKS = 6
WEIGHT_LOADS = 14
CHUNK_ROWS = [0, 512, 768, 128, 640, 896]
RH = D // 2


class At:

    def __init__(self, j, u, unroll):
        self.j, self.u, self.unroll = j, u, unroll

    def __add__(self, off):
        return At(self.j, self.u + off, self.unroll)

    def __sub__(self, off):
        return At(self.j, self.u - off, self.unroll)

    @property
    def n(self):
        return self.j * self.unroll + self.u

    def slot(self, ring):
        assert self.unroll % ring == 0
        return self.u % ring

    def turn(self, ring):
        return self.j * (self.unroll // ring) + self.u // ring

    def within(self, count):
        return not isinstance(self.j, int) or 0 <= self.n < count


def wait_from(eng, sem, value):
    if not isinstance(value, int) or value > 0:
        eng.wait_ge(sem, value)


def run_steps(eng, first, loop_from, loop_to, last, unroll, step):
    for n in range(first, loop_from):
        step(At(0, n, unroll))
    with eng.Fori(loop_from // unroll, loop_to // unroll) as j:
        for u in range(unroll):
            step(At(j, u, unroll))
    for n in range(loop_to, last):
        step(At(0, n, unroll))


def build(nc, x, src, dst, rel, w_rel, b_rel, w_ih, b_ih, b_hh, w1, b1, w2, b2, w3, b3, out):
    ctx = ExitStack()
    with ctx:
        ctx.enter_context(nc.allow_non_contiguous_dma(reason="bias columns, once"))

        def sb(name, shape, dt=F32):
            return ctx.enter_context(nc.sbuf_tensor(name, shape, dt))

        def sem(name):
            return ctx.enter_context(nc.semaphore(name))

        bank = [ctx.enter_context(nc.psum_tensor(f"bank{i}", [P, 512], F32)) for i in range(8)]

        agg = nc.dram_tensor("agg", (AGG_ROWS, D), F32).ap()
        dst_rows = nc.dram_tensor("dst_rows", (TILES, P), F32).ap()

        iotaf = sb("iotaf", [P, P])
        part_id = sb("part_id", [P, 1])
        ident = sb("ident", [P, P])
        ones = sb("ones", [P, P])
        ones16 = sb("ones16", [P, PAIR], F16)
        earlier = sb("earlier", [P, 3, P], F16)
        spare_row = sb("spare_row", [P, 2])
        pair_start = sb("pair_start", [1, BLOCKS, BLOCK_PAIRS])
        eps = sb("eps", [P, 1])

        src_slot = sb("src_slot", [P, TILES], I32)
        dst_slot = sb("dst_slot", [P, TILES])
        pair_rel = sb("pair_rel", [1, PAIRS], I32)

        REL_W = KH * 2 * D
        relT = sb("relT", [P, NUM_REL * REL_W], F16)
        relT_v = relT[:, :].rearrange("p (r k s o) -> p r k s o", r=NUM_REL, k=KH, s=2)
        ihT = sb("ihT", [P, KH, 2, CHUNKS * P], F32R)
        w1T = sb("w1T", [P, 2, KH * RH], F16)
        w2T = sb("w2T", [P, 2, RH], F16)
        w3T = sb("w3T", [P, 2, D], F16)
        brel_parts = sb("brel_parts", [P, NUM_REL * D], F16)
        bih_col = sb("bih_col", [P, 8])
        bhh_col = sb("bhh_col", [P, 8])
        gate_b = sb("gate_b", [P, 8])
        b1_col = sb("b1_col", [P, 1])
        b2_col = sb("b2_col", [P, 1])
        b3_all = sb("b3_all", [P, D])

        src_ring = sb("src_ring", [P, 4, 2], I32)
        dst_ring = sb("dst_ring", [P, 4, PAIR])
        xg = sb("xg", [P, 4, 2, D])
        stats = sb("stats", [P, 2, 2, 6])
        mean_var = sb("mean_var", [P, 4, 2, 2])
        std = sb("std", [P, 2, 2])
        rstd = sb("rstd", [P, 2, 2])
        shift = sb("shift", [P, 2, 2])
        xn = sb("xn", [P, 2, 2, D])
        s_hi = sb("s_hi", [P, 2, KH * PAIR], F16)
        s_lo = sb("s_lo", [P, 2, KH * PAIR], F16)
        h_hi = sb("h_hi", [P, 2, KH * PAIR], F16)
        h_lo = sb("h_lo", [P, 2, KH * PAIR], F16)
        m_hi = sb("m_hi", [P, 2, 2 * D], F16)
        m_lo = sb("m_lo", [P, 2, 2 * D], F16)
        same = sb("same", [P, 2, 3, P], F16)
        same_before = sb("same_before", [P, 2, 3, P], F16)
        count_tmp = sb("count_tmp", [P, 2, 3, P], F16)
        before = sb("before", [P, 4, 2])
        idx_f = sb("idx_f", [P, 4, 2])
        scatter_idx = sb("scatter_idx", [P, 4, 2], I32)
        summed = sb("summed", [P, 2, 2, D])

        prep_ctx = ExitStack()

        def tmp(name, shape, dt=F32):
            return prep_ctx.enter_context(nc.sbuf_tensor(name, shape, dt))

        upper = tmp("upper", [P, P])
        zeros = tmp("zeros", [P, ZERO_W])
        edge_i = tmp("edge_i", [ROWS, 3, BLOCKS, COLS], I32)
        rel_f = tmp("rel_f", [ROWS, BLOCKS, COLS])
        is_rel = tmp("is_rel", [ROWS, 2, BLOCKS, COLS])
        cum = tmp("cum", [ROWS, 2, BLOCKS, COLS])
        row_total = tmp("row_total", [ROWS, 2 * BLOCKS])
        prefix = tmp("prefix", [P, 4 * BLOCKS])
        slot_a = tmp("slot_a", [ROWS, BLOCKS, COLS])
        slot_b = tmp("slot_b", [ROWS, BLOCKS, COLS])
        slot_i = tmp("slot_i", [ROWS, BLOCKS, COLS], I32)
        tile_i = tmp("tile_i", [ROWS, BLOCKS, COLS], I32)
        tile16 = tmp("tile16", [ROWS, BLOCKS * COLS], F16)
        lane16 = tmp("lane16", [ROWS, BLOCKS * COLS], F16)
        parts_i = tmp("parts_i", [ROWS, PARTS, BLOCKS * COLS], I32)
        mixed_i = tmp("mixed_i", [ROWS, 2, BLOCKS * COLS], I32)
        dst_1 = tmp("dst_1", [ROWS, BLOCKS * COLS], I32)
        parts16 = tmp("parts16", [ROWS, PARTS, BLOCKS * COLS], F16)
        iota16 = tmp("iota16", [ROWS, P, BATCH], F16)
        hot_lane = tmp("hot_lane", [ROWS, 2, P, BATCH], F16)
        hot_is = tmp("hot_is", [ROWS, 2, BLOCK_TILES, BATCH], F16)
        hot_tile = tmp("hot_tile", [ROWS, 2, PARTS, BLOCK_TILES, BATCH], F16)
        placed = tmp("placed", [P, PARTS, BLOCKS * BLOCK_TILES], I32)
        src_rest = tmp("src_rest", [P, BLOCKS * BLOCK_TILES], I32)
        dst_high = tmp("dst_high", [P, BLOCKS * BLOCK_TILES], I32)
        dst_plus = tmp("dst_plus", [P, BLOCKS * BLOCK_TILES])
        dst_mark = tmp("dst_mark", [P, BLOCKS * BLOCK_TILES])
        dst_row_sb = tmp("dst_row_sb", [BLOCK_TILES, BLOCKS, P])
        rel_nat = tmp("rel_nat", [P, NUM_REL, KH, D])
        ih_nat = tmp("ih_nat", [P, CHUNKS, D])
        w1_nat = tmp("w1_nat", [P, D])
        w2_nat = tmp("w2_nat", [P, RH])
        w3_nat = tmp("w3_nat", [P, KH, RH])
        brel_row = tmp("brel_row", [2, NUM_REL * D])
        brel_hi = tmp("brel_hi", [2, NUM_REL * D], F16)
        prep_ctx.close()

        agg_in = sb("agg_in", [P, 2, UT, D])
        x_in = sb("x_in", [P, 2, UT, D])
        xb = sb("xb", [P, 2, UT, D])
        a_hi = sb("a_hi", [P, 2, KH, UNIT], F32R)
        a_lo = sb("a_lo", [P, 2, KH, UNIT], F32R)
        g_i = sb("g_i", [P, 2, UNIT])
        g_g = sb("g_g", [P, 2, UNIT])
        g_o = sb("g_o", [P, 2, UNIT])
        cell = sb("cell", [P, 2, UNIT])
        tcell = sb("tcell", [P, 2, UNIT])
        hn = sb("hn", [P, 2, UNIT])
        hn_hi = sb("hn_hi", [P, 2, KH, UNIT], F16)
        hn_lo = sb("hn_lo", [P, 2, KH, UNIT], F16)
        x1 = sb("x1", [P, UNIT])
        x1_hi = sb("x1_hi", [P, UNIT], F16)
        x1_lo = sb("x1_lo", [P, UNIT], F16)
        x2 = sb("x2", [P, UNIT])
        x2_hi = sb("x2_hi", [P, UNIT], F16)
        x2_lo = sb("x2_lo", [P, UNIT], F16)
        y = sb("y", [P, 2, UT, D])

        edges_in = sem("edges_in")
        weights_in = sem("weights_in")
        consts = sem("consts")
        zero_tile = sem("zero_tile")
        agg_zeroed = sem("agg_zeroed")
        prep = sem("prep")
        totals_ready = sem("totals_ready")
        prefix_ready = sem("prefix_ready")
        prefix_read = sem("prefix_read")
        hot_is_ready = sem("hot_is_ready")
        iota_ready = sem("iota_ready")
        hot_ready = sem("hot_ready")
        hot_last_ready = sem("hot_last_ready")
        hot_used = sem("hot_used")
        block_placed = sem("block_placed")
        block_out = sem("block_out")
        pair_rel_ready = sem("pair_rel_ready")
        src_slots_ready = sem("src_slots_ready")
        dst_slots_ready = sem("dst_slots_ready")
        dst_turned = sem("dst_turned")
        dst_row_ready = sem("dst_row_ready")
        dst_rows_stored = sem("dst_rows_stored")
        ident_ready = sem("ident_ready")
        w_turned = sem("w_turned")
        w_hi = sem("w_hi")
        w_lo = sem("w_lo")
        bias_ready = sem("bias_ready")

        src_loaded = [sem(f"src_loaded{i}") for i in range(4)]
        dst_loaded = [sem(f"dst_loaded{i}") for i in range(4)]
        gathered = [sem(f"gathered{i}") for i in range(4)]
        scattered = sem("scattered")
        gathers_cleared = sem("gathers_cleared")
        scatters_cleared = sem("scatters_cleared")
        stats_ready = sem("stats_ready")
        shift_ready = sem("shift_ready")
        var_ready = sem("var_ready")
        std_ready = sem("std_ready")
        rstd_ready = sem("rstd_ready")
        normed = sem("normed")
        s_turned = sem("s_turned")
        s_hi_ready = sem("s_hi_ready")
        s_ready = sem("s_ready")
        h_done = sem("h_done")
        h_hi_ready = sem("h_hi_ready")
        h_ready = sem("h_ready")
        m_done = sem("m_done")
        m_hi_ready = sem("m_hi_ready")
        m_ready = sem("m_ready")
        same_ready = sem("same_ready")
        same_before_ready = sem("same_before_ready")
        before_ready = sem("before_ready")
        idx_f_ready = sem("idx_f_ready")
        idx_ready = sem("idx_ready")
        sum_done = sem("sum_done")
        summed_ready = sem("summed_ready")

        agg_loaded = [sem(f"agg_loaded{i}") for i in range(2)]
        x_loaded = [sem(f"x_loaded{i}") for i in range(2)]
        stored = [sem(f"stored{i}") for i in range(2)]
        a_turned = sem("a_turned")
        a_hi_ready = sem("a_hi_ready")
        a_ready = sem("a_ready")
        chunk_done = sem("chunk_done")
        gate_ready = sem("gate_ready")
        cell_ready = sem("cell_ready")
        tcell_ready = sem("tcell_ready")
        hn_f_ready = sem("hn_f_ready")
        hn_hi_ready = sem("hn_hi_ready")
        hn_ready = sem("hn_ready")
        x1_done = sem("x1_done")
        x1_f_ready = sem("x1_f_ready")
        x1_hi_ready = sem("x1_hi_ready")
        x1_ready = sem("x1_ready")
        x2_done = sem("x2_done")
        x2_f_ready = sem("x2_f_ready")
        x2_hi_ready = sem("x2_hi_ready")
        x2_ready = sem("x2_ready")
        y_done = sem("y_done")
        xb_ready = sem("xb_ready")
        y_ready = sem("y_ready")

        def weight_groups():
            groups = []
            for r in range(NUM_REL):
                groups.append(([rel_nat[:, r, oc, k * P:(k + 1) * P] for k in range(KH) for oc in range(KH)],
                               [(0, KH * D, relT_v[:, r, :, 0, :], relT_v[:, r, :, 1, :], KH)]))
            half = CHUNKS // 2 * P
            for k in range(KH):
                for part in range(2):
                    cs = range(part * CHUNKS // 2, (part + 1) * CHUNKS // 2)
                    cols = slice(part * half, (part + 1) * half)
                    groups.append(([ih_nat[:, c, k * P:(k + 1) * P] for c in cs],
                                   [(0, half, ihT[:, k, 0, cols], ihT[:, k, 1, cols], 1)]))
            groups.append(([w1_nat[:, k * P:(k + 1) * P] for k in range(KH)] + [w2_nat[:, :]],
                           [(0, KH * RH, w1T[:, 0, :], w1T[:, 1, :], 1),
                            (KH * RH, KH * RH + RH, w2T[:, 0, :], w2T[:, 1, :], 1)]))
            groups.append(([w3_nat[:, oc, :] for oc in range(KH)], [(0, D, w3T[:, 0, :], w3T[:, 1, :], 1)]))
            return groups

        GROUPS = weight_groups()
        W_BANK = [bank[4 + g % 4] for g in range(len(GROUPS))]

        def part_view(b, lo, hi, k):
            v = b[:, lo:hi]
            return v.rearrange("p (k o) -> p k o", k=k) if k > 1 else v

        def plain(ap):
            return ap.bitcast(F32) if ap.dtype == F32R else ap

        B_T, B_H, B_M, B_G = (bank[0:2], bank[2:4], bank[4:6], bank[6:8])
        N_T, N_C, N_X, N_Y = (bank[0:2], bank[2:5], bank[5], bank[6:8])

        EDGE_RUN = dict(loop_from=8, loop_to=PAIRS - 8, unroll=4)
        NODE_RUN = dict(loop_from=4, loop_to=UNITS - 4, unroll=2)

        def unit_rows(u):
            return min(u * UNIT, NODES - UNIT) if isinstance(u, int) else u * UNIT

        def unit_view(t, u):
            return t[bass.ds(unit_rows(u), UNIT), :].rearrange("(p t) d -> p t d", t=UT)

        block = ctx.enter_context(nc.Block())

        @block.sync
        def _(sp):
            for i, t in enumerate((src, dst, rel)):
                sp.dma_start(edge_i[:, i, :, :], t.rearrange("(b p c) -> p b c", b=BLOCKS, c=COLS)).then_inc(edges_in, 16)
            for r in range(NUM_REL):
                sp.dma_start(rel_nat[:, r, :, :], w_rel[r, :, :].rearrange("(c p) i -> p c i", p=P)).then_inc(weights_in, 16)
            for c in range(CHUNKS // KH):
                row = CHUNK_ROWS[c]
                sp.dma_start(ih_nat[:, c::CHUNKS // KH, :],
                             w_ih[row:row + D, :].rearrange("(h p) i -> p h i", p=P)).then_inc(weights_in, 16)
            sp.dma_start(w1_nat[:, :], w1).then_inc(weights_in, 16)
            sp.dma_start(w2_nat[:, :], w2).then_inc(weights_in, 16)
            sp.dma_start(w3_nat[:, :, :], w3.rearrange("(c p) i -> p c i", p=P)).then_inc(weights_in, 16)
            sp.wait_ge(src_slots_ready, 1)

            def step(at):
                k = at + 6
                if k.within(PAIRS):
                    wait_from(sp, gathered[k.slot(4)], k.turn(4) * 32)
                    sp.dma_start(src_ring[:, k.slot(4), :],
                                 src_slot[:, bass.ds(k.n * 2, 2)]).then_inc(src_loaded[k.slot(4)], 16)
                k = at
                if isinstance(k.n, int) and k.n == 0:
                    sp.wait_ge(dst_row_ready, 1)
                    sp.dma_start(dst_rows.rearrange("(b t) p -> t b p", b=BLOCKS),
                                 dst_row_sb[:, :, :]).then_inc(dst_rows_stored, 16)
                    sp.wait_ge(dst_rows_stored, 16)
                if k.within(PAIRS):
                    wait_from(sp, same_ready, k.n - 3)
                    sp.dma_start(dst_ring[:, k.slot(4), :],
                                 dst_rows[bass.ds(k.n * 2, 2), :].rearrange("t p -> (t p)").partition_broadcast(P)
                                 ).then_inc(dst_loaded[k.slot(4)], 16)

            run_steps(sp, -6, last=PAIRS, step=step, **EDGE_RUN)

            sp.wait_ge(scattered, 32 * PAIRS)

            def node_step(at):
                k = at + 2
                if k.within(UNITS):
                    wait_from(sp, a_turned, k.n - 1)
                    sp.dma_start(agg_in[:, k.slot(2), :, :], unit_view(agg, k.n)).then_inc(agg_loaded[k.slot(2)], 16)
                k = at
                if k.within(UNITS):
                    wait_from(sp, xb_ready, k.n - 1)
                    sp.dma_start(x_in[:, k.slot(2), :, :], unit_view(x, k.n)).then_inc(x_loaded[k.slot(2)], 16)
                k = at - 3
                if k.within(UNITS):
                    sp.wait_ge(y_ready, k.n + 1)
                    if isinstance(k.n, int) and k.n == UNITS - 1:
                        sp.wait_ge(stored[(k - 1).slot(2)], 16 * ((k - 1).turn(2) + 1))
                    sp.dma_start(unit_view(out, k.n), y[:, k.slot(2), :, :]).then_inc(stored[k.slot(2)], 16)

            run_steps(sp, -2, last=UNITS + 3, step=node_step, **NODE_RUN)
            for s in range(2):
                sp.wait_ge(stored[s], 16 * len(range(s, UNITS, 2)))

        @block.gpsimd
        def _(pool):
            nc.gpsimd.iota(iotaf[:, :], [[1, P]], base=0, channel_multiplier=0,
                           allow_small_or_imprecise_dtypes=True)
            nc.gpsimd.iota(part_id[:, :], [[1, 1]], base=0, channel_multiplier=1,
                           allow_small_or_imprecise_dtypes=True)
            nc.gpsimd.iota(spare_row[:, :], [[P, 2]], base=NODES, channel_multiplier=1,
                           allow_small_or_imprecise_dtypes=True)
            nc.gpsimd.iota(pair_start[:, :, :], [[0, BLOCKS], [PAIR, BLOCK_PAIRS]], base=0, channel_multiplier=0,
                           allow_small_or_imprecise_dtypes=True)
            nc.gpsimd.memset(ones[:, :], 1.0)
            nc.gpsimd.memset(ones16[:, :], 1.0)
            nc.gpsimd.memset(eps[:, :], LN_EPS).then_inc(consts, 1)

            def times_last_part(n, q):
                pool.wait_ge(hot_is_ready, n + 1)
                wait_from(pool, hot_used, n - 1)
                nc.gpsimd.tensor_tensor(hot_tile[:, q, PARTS - 1, :, :], hot_is[:, q, :, :],
                                        parts16[:, PARTS - 1, bass.ds(n * BATCH, BATCH)].unsqueeze(1).to_broadcast(
                                            [ROWS, BLOCK_TILES, BATCH]), ALU.mult).then_inc(hot_last_ready, 1)

            times_last_part(0, 0)
            times_last_part(1, 1)
            with pool.Fori(1, BLOCKS * BATCHES // 2) as g:
                for q in range(2):
                    times_last_part(g * 2 + q, q)

            def step(at):
                k = at - 4
                if k.within(PAIRS):
                    pool.wait_ge(idx_ready, k.n + 1)
                    pool.wait_ge(summed_ready, k.n + 1)
                    if isinstance(k.n, int) and k.n == 0:
                        pool.wait_ge(agg_zeroed, 16 * ZERO_DMAS)
                    wait_from(pool, scattered, k.n * 32)
                    pool.sem_inc(scatters_cleared, 1)
                    for t in range(2):
                        nc.gpsimd.indirect_dma_start(
                            out=agg[:, :],
                            out_offset=bass.IndirectOffsetOnAxis(ap=scatter_idx[:, k.slot(4), t:t + 1], axis=0),
                            in_=summed[:, k.slot(2), t, :], in_offset=None, compute_op=ALU.add).then_inc(scattered, 16)
                k = at + 4
                if k.within(PAIRS):
                    pool.wait_ge(src_loaded[k.slot(4)], 16 * (k.turn(4) + 1))
                    wait_from(pool, normed, k.n - 3)
                    pool.sem_inc(gathers_cleared, 1)
                    for t in range(2):
                        nc.gpsimd.indirect_dma_start(
                            out=xg[:, k.slot(4), t, :], out_offset=None, in_=x[:, :],
                            in_offset=bass.IndirectOffsetOnAxis(ap=src_ring[:, k.slot(4), t:t + 1], axis=0)
                        ).then_inc(gathered[k.slot(4)], 16)

            run_steps(pool, -4, last=PAIRS + 4, step=step, **EDGE_RUN)

            pool.wait_ge(weights_in, 16 * WEIGHT_LOADS)

            def node_step(at):
                k = at - 1
                if k.within(UNITS):
                    pool.wait_ge(x_loaded[k.slot(2)], 16 * (k.turn(2) + 1))
                    wait_from(pool, y_ready, k.n - 1)
                    nc.gpsimd.tensor_tensor(xb[:, k.slot(2), :, :], x_in[:, k.slot(2), :, :],
                                            b3_all[:, :].unsqueeze(1).to_broadcast([P, UT, D]), ALU.add).then_inc(xb_ready, 1)

            run_steps(pool, 1, last=UNITS + 1, step=node_step, **NODE_RUN)

        @block.scalar
        def _(act):
            act.dma_start(brel_row[:, :], b_rel.rearrange("r d -> (r d)").partition_broadcast(2)).then_inc(weights_in, 16)
            act.dma_start(bih_col[:, :], b_ih.rearrange("(c p) -> p c", p=P)).then_inc(weights_in, 16)
            act.dma_start(bhh_col[:, :], b_hh.rearrange("(c p) -> p c", p=P)).then_inc(weights_in, 16)
            act.dma_start(b1_col[:, :], b1.rearrange("(p c) -> p c", c=1)).then_inc(weights_in, 16)
            act.dma_start(b2_col[:, :], b2.rearrange("(p c) -> p c", c=1)).then_inc(weights_in, 16)
            act.dma_start(b3_all[:, :], b3.partition_broadcast(P)).then_inc(weights_in, 16)
            act.wait_ge(zero_tile, 1)
            act.wait_ge(edges_in, 48)
            act.wait_ge(weights_in, 16 * WEIGHT_LOADS)
            agg_z = agg.rearrange("(p r) d -> p (r d)", p=P).rearrange("p (n w) -> p n w", w=ZERO_W)
            per = ZERO_REPS // ZERO_DMAS
            for i in range(ZERO_DMAS):
                act.dma_start(agg_z[:, i * per:(i + 1) * per, :],
                              zeros[:, :].unsqueeze(1).to_broadcast([P, per, ZERO_W])).then_inc(agg_zeroed, 16)
            act.wait_ge(consts, 1)
            nc.scalar.copy(iota16[:, :, :], iotaf[0:ROWS, :].unsqueeze(2).to_broadcast([ROWS, P, BATCH])).then_inc(iota_ready, 1)
            for g, (_, targets) in enumerate(GROUPS):
                act.wait_ge(w_turned, g + 1)
                for lo, hi, to_hi, _, k in targets:
                    last = nc.scalar.copy(to_hi, part_view(W_BANK[g], lo, hi, k))
                last.then_inc(w_hi, 1)
            for b in range(BLOCKS):
                act.wait_ge(block_placed, b + 1)
                nc.scalar.copy(placed[:, :, b * BLOCK_TILES:(b + 1) * BLOCK_TILES],
                               bank[b][:, 0:PARTS * BLOCK_TILES].rearrange("p (n t) -> p n t", n=PARTS)).then_inc(block_out, 1)

            def step(at):
                k = at - 4
                if k.within(PAIRS):
                    act.wait_ge(sum_done, k.n + 1)
                    wait_from(act, scattered, (k.n - 1) * 32)
                    nc.scalar.copy(summed[:, k.slot(2), :, :].rearrange("p t d -> p (t d)"),
                                   B_G[k.slot(2)][:, :]).then_inc(summed_ready, 1)
                k = at
                if k.within(PAIRS):
                    act.wait_ge(s_turned, k.n + 1)
                    nc.scalar.activation(s_hi[:, k.slot(2), :], B_T[k.slot(2)][:, :], ACT.Relu).then_inc(s_hi_ready, 1)
                k = at - 3
                if k.within(PAIRS):
                    act.wait_ge(same_before_ready, k.n + 1)
                    nc.scalar.activation(count_tmp[:, k.slot(2), 0, :], same_before[:, k.slot(2), 0, :], ACT.Copy,
                                         accum_out=before[:, k.slot(4), 0:1])
                    nc.scalar.activation(count_tmp[:, k.slot(2), 1:3, :], same_before[:, k.slot(2), 1:3, :], ACT.Copy,
                                         accum_out=before[:, k.slot(4), 1:2]).then_inc(before_ready, 1)
                k = at + 2
                if k.within(PAIRS):
                    act.wait_ge(var_ready, k.n + 1)
                    nc.scalar.activation(std[:, k.slot(2), :], mean_var[:, k.slot(4), :, 1], ACT.Sqrt,
                                         bias=eps[:, 0:1]).then_inc(std_ready, 1)
                k = at - 1
                if k.within(PAIRS):
                    act.wait_ge(h_done, k.n + 1)
                    nc.scalar.activation(h_hi[:, k.slot(2), :], B_H[k.slot(2)][:, :], ACT.Relu).then_inc(h_hi_ready, 1)
                k = at + 1
                if k.within(PAIRS):
                    act.wait_ge(shift_ready, k.n + 1)
                    for t in range(2):
                        last = nc.scalar.activation(xn[:, k.slot(2), t, :], xg[:, k.slot(4), t, :], ACT.Identity,
                                                    bias=shift[:, k.slot(2), t:t + 1], scale=rstd[:, k.slot(2), t:t + 1])
                    last.then_inc(normed, 1)
                k = at - 2
                if k.within(PAIRS):
                    act.wait_ge(m_done, k.n + 1)
                    nc.scalar.activation(m_hi[:, k.slot(2), :], B_M[k.slot(2)][:, :], ACT.Relu).then_inc(m_hi_ready, 1)

            run_steps(act, -2, last=PAIRS + 4, step=step, **EDGE_RUN)

            def gate(k, c):
                half = c // 3
                to, fn = ((g_i, ACT.Sigmoid), (g_g, ACT.Tanh), (g_o, ACT.Sigmoid))[c % 3]
                act.wait_ge(chunk_done, k.n * CHUNKS + c + 1)
                col = CHUNK_ROWS[c] // P
                nc.scalar.activation(to[:, half, :], N_C[c % 3][:, :], fn,
                                     bias=gate_b[:, col:col + 1]).then_inc(gate_ready, 1)

            def tanh_cell(k, half):
                act.wait_ge(cell_ready, k.n * KH + half + 1)
                nc.scalar.activation(tcell[:, half, :], cell[:, half, :], ACT.Tanh).then_inc(tcell_ready, 1)

            def node_step(at):
                if at.within(UNITS):
                    for c in range(3):
                        gate(at, c)
                    tanh_cell(at, 0)
                k = at - 1
                if k.within(UNITS):
                    act.wait_ge(x1_done, k.n + 1)
                    nc.scalar.activation(x1[:, :], N_X[:, :], ACT.Relu, bias=b1_col[:, 0:1]).then_inc(x1_f_ready, 1)
                if at.within(UNITS):
                    gate(at, 3)
                k = at + 1
                if k.within(UNITS):
                    act.wait_ge(a_turned, k.n + 1)
                    for h in range(KH):
                        nc.scalar.copy(a_hi[:, k.slot(2), h, :], N_T[h][:, :]).then_inc(a_hi_ready, 1)
                if at.within(UNITS):
                    gate(at, 4)
                k = at - 1
                if k.within(UNITS):
                    act.wait_ge(x2_done, k.n + 1)
                    nc.scalar.activation(x2[:, :], N_X[:, :], ACT.Relu, bias=b2_col[:, 0:1]).then_inc(x2_f_ready, 1)
                if at.within(UNITS):
                    gate(at, 5)
                    tanh_cell(at, 1)

            run_steps(act, -1, last=UNITS + 1, step=node_step, **NODE_RUN)

        @block.vector
        def _(dve):
            done = [0]

            def chained(ins):
                done[0] += 1
                ins.then_inc(prep, 1)
                dve.wait_ge(prep, done[0])

            nc.vector.memset(zeros[:, :], 0.0).then_inc(zero_tile, 1)
            dve.wait_ge(consts, 1)
            nc.vector.tensor_scalar(ident[:, :], iotaf[:, :], part_id[:, 0:1], None, ALU.is_equal)
            nc.vector.tensor_scalar(upper[:, :], iotaf[:, :], part_id[:, 0:1], None, ALU.is_gt).then_inc(ident_ready, 1)
            nc.vector.memset(earlier[:, 1, :], 1.0)
            for tile in (0, 2):
                nc.vector.tensor_scalar(earlier[:, tile, :], iotaf[:, :], part_id[:, 0:1], None, ALU.is_lt)
            nc.vector.memset(brel_parts[:, :], 0.0)

            dve.wait_ge(edges_in, 48)
            chained(nc.vector.tensor_copy(rel_f[:, :, :], edge_i[:, 2, :, :]))
            for r in range(NUM_REL):
                last = nc.vector.tensor_scalar(is_rel[:, r, :, :], rel_f[:, :, :], float(r), None, ALU.is_equal)
            chained(last)
            for r in range(NUM_REL):
                for b in range(BLOCKS):
                    last = nc.vector.tensor_tensor_scan(cum[:, r, b, :], is_rel[:, r, b, :], zeros[0:ROWS, 0:COLS], 0.0,
                                                        ALU.add, ALU.add)
            chained(last)
            nc.vector.tensor_copy(row_total[:, :].rearrange("p (r b) -> p r b", r=2), cum[:, :, :, COLS - 1]).then_inc(totals_ready, 1)
            src_i = edge_i[:, 0, :, :].rearrange("p b c -> p (b c)")
            nc.vector.tensor_scalar(parts_i[:, 0, :], src_i, SRC_LOW, None, ALU.arith_shift_right)
            nc.vector.tensor_scalar(mixed_i[:, 0, :], src_i, (1 << SRC_LOW) - 1, DST_HIGH, ALU.bitwise_and,
                                    ALU.logical_shift_left)
            chained(nc.vector.tensor_scalar(dst_1[:, :], edge_i[:, 1, :, :].rearrange("p b c -> p (b c)"), 1, None, ALU.add))
            nc.vector.tensor_scalar(parts_i[:, 2, :], dst_1[:, :], (1 << DST_LOW) - 1, None, ALU.bitwise_and)
            chained(nc.vector.tensor_scalar(mixed_i[:, 1, :], dst_1[:, :], DST_LOW, None, ALU.arith_shift_right))
            chained(nc.vector.tensor_tensor(parts_i[:, 1, :], mixed_i[:, 0, :], mixed_i[:, 1, :], ALU.add))
            dve.wait_ge(prefix_ready, 1)
            nc.vector.tensor_copy(prefix[:, :], bank[0][:, 0:4 * BLOCKS]).then_inc(prefix_read, 1)
            dve.wait_ge(prefix_read, 1)
            nc.vector.tensor_tensor(pair_rel[:, :].rearrange("p (b q) -> p b q", b=BLOCKS), pair_start[:, :, :],
                                    prefix[0:1, 2 * BLOCKS:3 * BLOCKS].unsqueeze(2).to_broadcast([1, BLOCKS, BLOCK_PAIRS]),
                                    ALU.is_ge).then_inc(pair_rel_ready, 1)
            for b in range(BLOCKS):
                nc.vector.tensor_scalar(slot_a[:, b, :], cum[:, 0, b, :], prefix[0:ROWS, b:b + 1],
                                        -1.0 - BLOCK_SLOTS, ALU.add, ALU.add)
                last = nc.vector.tensor_scalar(slot_b[:, b, :], cum[:, 1, b, :], prefix[0:ROWS, BLOCKS + b:BLOCKS + b + 1],
                                               -1.0, ALU.add, ALU.mult)
            chained(last)
            nc.vector.tensor_tensor(slot_a[:, :, :], slot_a[:, :, :], is_rel[:, 0, :, :], ALU.mult)
            chained(nc.vector.tensor_tensor(slot_b[:, :, :], slot_b[:, :, :], is_rel[:, 1, :, :], ALU.mult))
            chained(nc.vector.scalar_tensor_tensor(out=slot_i[:, :, :].rearrange("p b c -> p (b c)"),
                                                   in0=slot_a[:, :, :].rearrange("p b c -> p (b c)"),
                                                   scalar=float(BLOCK_SLOTS),
                                                   in1=slot_b[:, :, :].rearrange("p b c -> p (b c)"),
                                                   op0=ALU.add, op1=ALU.add))
            chained(nc.vector.tensor_scalar(tile_i[:, :, :], slot_i[:, :, :], 7, None, ALU.arith_shift_right))
            chained(nc.vector.tensor_copy(tile16[:, :], tile_i[:, :, :].rearrange("p b c -> p (b c)")))
            chained(nc.vector.tensor_scalar(tile_i[:, :, :], slot_i[:, :, :], P - 1, None, ALU.bitwise_and))
            nc.vector.tensor_copy(parts16[:, :, :], parts_i[:, :, :])
            chained(nc.vector.tensor_copy(lane16[:, :], tile_i[:, :, :].rearrange("p b c -> p (b c)")))

            for g, (_, targets) in enumerate(GROUPS):
                dve.wait_ge(w_hi, g + 1)
                for lo, hi, to_hi, to_lo, k in targets:
                    last = nc.vector.tensor_tensor(to_lo, part_view(W_BANK[g], lo, hi, k), plain(to_hi), ALU.subtract)
                last.then_inc(w_lo, 1)
            dve.wait_ge(weights_in, 16 * WEIGHT_LOADS)
            nc.vector.tensor_tensor(gate_b[:, :], bih_col[:, :], bhh_col[:, :], ALU.add)
            chained(nc.vector.tensor_copy(brel_hi[:, :], brel_row[:, :]))
            chained(nc.vector.tensor_tensor(brel_parts[0:2, :], brel_row[:, :], brel_hi[:, :], ALU.subtract))
            nc.vector.tensor_copy(brel_parts[0:1, :], brel_hi[0:1, :]).then_inc(bias_ready, 1)

            def over(ap, width):
                return ap.unsqueeze(1).to_broadcast([ROWS, width, BATCH])

            def is_tile(n, q):
                wait_from(dve, hot_ready, n - 1)
                wait_from(dve, hot_last_ready, n - 1)
                nc.vector.tensor_tensor(hot_is[:, q, :, :], iota16[:, 0:BLOCK_TILES, :],
                                        over(tile16[:, bass.ds(n * BATCH, BATCH)], BLOCK_TILES),
                                        ALU.is_equal).then_inc(hot_is_ready, 1)

            def times_parts(n, q):
                dve.wait_ge(hot_is_ready, n + 1)
                wait_from(dve, hot_used, n - 1)
                for i in range(PARTS - 1):
                    nc.vector.tensor_tensor(hot_tile[:, q, i, :, :], hot_is[:, q, :, :],
                                            over(parts16[:, i, bass.ds(n * BATCH, BATCH)], BLOCK_TILES), ALU.mult)
                nc.vector.tensor_tensor(hot_lane[:, q, :, :], iota16[:, :, :],
                                        over(lane16[:, bass.ds(n * BATCH, BATCH)], P),
                                        ALU.is_equal).then_inc(hot_ready, 1)

            dve.wait_ge(iota_ready, 1)
            is_tile(0, 0)
            for n in range(2):
                is_tile(n + 1, (n + 1) % 2)
                times_parts(n, n % 2)
            with dve.Fori(1, BLOCKS * BATCHES // 2 - 1) as g:
                for q in range(2):
                    is_tile(g * 2 + q + 1, (q + 1) % 2)
                    times_parts(g * 2 + q, q)
            is_tile(BLOCKS * BATCHES - 1, 1)
            for n in range(BLOCKS * BATCHES - 2, BLOCKS * BATCHES):
                times_parts(n, n % 2)

            dve.wait_ge(block_out, BLOCKS)
            nc.vector.tensor_scalar(src_rest[:, :], placed[:, 1, :], DST_HIGH, None, ALU.arith_shift_right)
            chained(nc.vector.tensor_scalar(dst_high[:, :], placed[:, 1, :], (1 << DST_HIGH) - 1, None, ALU.bitwise_and))
            nc.vector.scalar_tensor_tensor(out=src_slot[:, :], in0=placed[:, 0, :], scalar=float(1 << SRC_LOW),
                                           in1=src_rest[:, :], op0=ALU.mult, op1=ALU.add).then_inc(src_slots_ready, 1)
            chained(nc.vector.scalar_tensor_tensor(out=dst_plus[:, :], in0=dst_high[:, :], scalar=float(1 << DST_LOW),
                                                   in1=placed[:, 2, :], op0=ALU.mult, op1=ALU.add))
            chained(nc.vector.tensor_scalar(dst_mark[:, :], dst_plus[:, :], 0.0, FAR, ALU.is_equal, ALU.mult))
            nc.vector.scalar_tensor_tensor(out=dst_slot[:, :], in0=dst_plus[:, :], scalar=-1.0,
                                           in1=dst_mark[:, :], op0=ALU.add, op1=ALU.add).then_inc(dst_slots_ready, 1)
            dve.wait_ge(dst_turned, 1)
            for b in range(BLOCKS):
                last = nc.vector.tensor_copy(dst_row_sb[:, b, :], bank[4][0:BLOCK_TILES, b * P:(b + 1) * P])
            last.then_inc(dst_row_ready, 1)
            dve.wait_ge(dst_slots_ready, 1)

            def step(at):
                k = at + 2
                if k.within(PAIRS):
                    dve.wait_ge(stats_ready, k.n + 1)
                k = at - 3
                if k.within(PAIRS):
                    dve.wait_ge(m_hi_ready, k.n + 1)
                    nc.vector.scalar_tensor_tensor(out=m_lo[:, k.slot(2), :], in0=B_M[k.slot(2)][:, :], scalar=0.0,
                                                   in1=m_hi[:, k.slot(2), :], op0=ALU.max,
                                                   op1=ALU.subtract).then_inc(m_ready, 1)
                k = at + 2
                if k.within(PAIRS):
                    for t in range(2):
                        last = nc.vector.bn_aggr(mean_var[:, k.slot(4), t, :], stats[:, k.slot(2), t, :])
                    last.then_inc(var_ready, 1)
                k = at
                if k.within(PAIRS):
                    dve.wait_ge(s_hi_ready, k.n + 1)
                    nc.vector.scalar_tensor_tensor(out=s_lo[:, k.slot(2), :], in0=B_T[k.slot(2)][:, :], scalar=0.0,
                                                   in1=s_hi[:, k.slot(2), :], op0=ALU.max,
                                                   op1=ALU.subtract).then_inc(s_ready, 1)
                k = at - 2
                if k.within(PAIRS):
                    dve.wait_ge(dst_loaded[k.slot(4)], 16 * (k.turn(4) + 1))
                    if not at.within(PAIRS):
                        wait_from(dve, sum_done, k.n - 1)
                    nc.vector.tensor_scalar(same[:, k.slot(2), 0, :], dst_ring[:, k.slot(4), 0:P],
                                            dst_slot[:, bass.ds(k.n * 2, 1)], None, ALU.is_equal)
                    nc.vector.tensor_scalar(same[:, k.slot(2), 1:3, :].rearrange("p a b -> p (a b)"), dst_ring[:, k.slot(4), :],
                                            dst_slot[:, bass.ds(k.n * 2 + 1, 1)], None, ALU.is_equal).then_inc(same_ready, 1)
                k = at - 1
                if k.within(PAIRS):
                    dve.wait_ge(h_hi_ready, k.n + 1)
                    nc.vector.scalar_tensor_tensor(out=h_lo[:, k.slot(2), :], in0=B_H[k.slot(2)][:, :], scalar=0.0,
                                                   in1=h_hi[:, k.slot(2), :], op0=ALU.max,
                                                   op1=ALU.subtract).then_inc(h_ready, 1)
                k = at + 2
                if k.within(PAIRS):
                    dve.wait_ge(std_ready, k.n + 1)
                    nc.vector.reciprocal(rstd[:, k.slot(2), :], std[:, k.slot(2), :]).then_inc(rstd_ready, 1)
                k = at - 3
                if k.within(PAIRS):
                    dve.wait_ge(before_ready, k.n + 1)
                    nc.vector.scalar_tensor_tensor(out=idx_f[:, k.slot(4), :], in0=before[:, k.slot(4), :], scalar=SPARE,
                                                   in1=dst_slot[:, bass.ds(k.n * 2, 2)], op0=ALU.mult,
                                                   op1=ALU.add).then_inc(idx_f_ready, 1)
                k = at + 2
                if k.within(PAIRS):
                    dve.wait_ge(rstd_ready, k.n + 1)
                    nc.vector.scalar_tensor_tensor(out=shift[:, k.slot(2), :], in0=mean_var[:, k.slot(4), :, 0], scalar=-1.0,
                                                   in1=rstd[:, k.slot(2), :], op0=ALU.mult,
                                                   op1=ALU.mult).then_inc(shift_ready, 1)
                k = at + 3
                if k.within(PAIRS):
                    dve.wait_ge(gathered[k.slot(4)], 32 * (k.turn(4) + 1))
                    for t in range(2):
                        last = nc.vector.bn_stats(stats[:, k.slot(2), t, :], xg[:, k.slot(4), t, :])
                    last.then_inc(stats_ready, 1)
                k = at - 2
                if k.within(PAIRS):
                    dve.wait_ge(same_ready, k.n + 1)
                    nc.vector.tensor_tensor(same_before[:, k.slot(2), :, :].rearrange("p a b -> p (a b)"),
                                            same[:, k.slot(2), :, :].rearrange("p a b -> p (a b)"),
                                            earlier[:, :, :].rearrange("p a b -> p (a b)"),
                                            ALU.mult).then_inc(same_before_ready, 1)
                k = at - 3
                if k.within(PAIRS):
                    dve.wait_ge(idx_f_ready, k.n + 1)
                    nc.vector.tensor_tensor(scatter_idx[:, k.slot(4), :], idx_f[:, k.slot(4), :], spare_row[:, :],
                                            ALU.min).then_inc(idx_ready, 1)

            run_steps(dve, -3, last=PAIRS + 3, step=step, **EDGE_RUN)

            def cell_of(k, half):
                dve.wait_ge(gate_ready, k.n * CHUNKS + half * 3 + 2)
                nc.vector.tensor_tensor(cell[:, half, :], g_i[:, half, :], g_g[:, half, :], ALU.mult).then_inc(cell_ready, 1)

            def hidden(k, half):
                dve.wait_ge(tcell_ready, k.n * KH + half + 1)
                nc.vector.tensor_tensor(hn[:, half, :], g_o[:, half, :], tcell[:, half, :], ALU.mult).then_inc(hn_f_ready, 1)

            def hidden_hi(k, half):
                dve.wait_ge(hn_f_ready, k.n * KH + half + 1)
                nc.vector.tensor_copy(hn_hi[:, k.slot(2), half, :], hn[:, half, :]).then_inc(hn_hi_ready, 1)

            def hidden_lo(k, half):
                dve.wait_ge(hn_hi_ready, k.n * KH + half + 1)
                nc.vector.tensor_tensor(hn_lo[:, k.slot(2), half, :], hn[:, half, :], hn_hi[:, k.slot(2), half, :],
                                        ALU.subtract).then_inc(hn_ready, 1)

            def result(k, part):
                rows = slice(part * UT // 2, (part + 1) * UT // 2)
                if part == 0:
                    dve.wait_ge(y_done, k.n + 1)
                    dve.wait_ge(xb_ready, k.n + 1)
                    wait_from(dve, stored[k.slot(2)], 16 * k.turn(2))
                ins = nc.vector.tensor_tensor(y[:, k.slot(2), rows, :].rearrange("p t d -> p (t d)"), N_Y[part][:, :],
                                              xb[:, k.slot(2), rows, :].rearrange("p t d -> p (t d)"), ALU.add)
                if part == 1:
                    ins.then_inc(y_ready, 1)

            def node_step(at):
                if at.within(UNITS):
                    cell_of(at, 0)
                if (at - 2).within(UNITS):
                    result(at - 2, 0)
                if at.within(UNITS):
                    hidden(at, 0)
                if (at - 2).within(UNITS):
                    result(at - 2, 1)
                if at.within(UNITS):
                    hidden_hi(at, 0)
                k = at - 1
                if k.within(UNITS):
                    dve.wait_ge(x1_f_ready, k.n + 1)
                    nc.vector.tensor_copy(x1_hi[:, :], x1[:, :]).then_inc(x1_hi_ready, 1)
                if at.within(UNITS):
                    hidden_lo(at, 0)
                if k.within(UNITS):
                    dve.wait_ge(x1_hi_ready, k.n + 1)
                    nc.vector.tensor_tensor(x1_lo[:, :], x1[:, :], x1_hi[:, :], ALU.subtract).then_inc(x1_ready, 1)
                k = at + 1
                if k.within(UNITS):
                    for h in range(KH):
                        dve.wait_ge(a_hi_ready, k.n * KH + h + 1)
                        last = nc.vector.tensor_tensor(a_lo[:, k.slot(2), h, :], N_T[h][:, :],
                                                       plain(a_hi[:, k.slot(2), h, :]), ALU.subtract)
                    last.then_inc(a_ready, 1)
                if at.within(UNITS):
                    cell_of(at, 1)
                k = at - 1
                if k.within(UNITS):
                    dve.wait_ge(x2_f_ready, k.n + 1)
                    nc.vector.tensor_copy(x2_hi[:, :], x2[:, :]).then_inc(x2_hi_ready, 1)
                    dve.wait_ge(x2_hi_ready, k.n + 1)
                    nc.vector.tensor_tensor(x2_lo[:, :], x2[:, :], x2_hi[:, :], ALU.subtract).then_inc(x2_ready, 1)
                if at.within(UNITS):
                    hidden(at, 1)
                    hidden_hi(at, 1)
                    hidden_lo(at, 1)

            run_steps(dve, -1, last=UNITS + 2, step=node_step, **NODE_RUN)

        @block.tensor
        def _(pe):
            pe.wait_ge(ident_ready, 1)
            pe.wait_ge(totals_ready, 1)
            nc.tensor.matmul(bank[0][:, 0:2 * BLOCKS], upper[0:ROWS, :], row_total[:, :], start=True, stop=True)
            nc.tensor.matmul(bank[0][:, 2 * BLOCKS:4 * BLOCKS], ones[0:ROWS, :], row_total[:, :],
                             start=True, stop=True).then_inc(prefix_ready, 1)
            pe.wait_ge(weights_in, 16 * WEIGHT_LOADS)
            for g, (blocks, _) in enumerate(GROUPS):
                wait_from(pe, w_lo, g - 3)
                for i, w in enumerate(blocks):
                    last = nc.tensor.transpose(W_BANK[g][:, i * P:(i + 1) * P], w, ident[:, :])
                last.then_inc(w_turned, 1)

            def place(n, b, q):
                pe.wait_ge(hot_ready, n + 1)
                pe.wait_ge(hot_last_ready, n + 1)
                for c in range(BATCH):
                    last = nc.tensor.matmul(bank[b][:, 0:PARTS * BLOCK_TILES], hot_lane[:, q, :, c],
                                            hot_tile[:, q, :, :, c].rearrange("p n t -> p (n t)"), start=False, stop=False)
                last.then_inc(hot_used, 1)

            def clear(b, start):
                return nc.tensor.matmul(bank[b][:, 0:PARTS * BLOCK_TILES], zeros[:, 0:P],
                                        zeros[:, 0:PARTS * BLOCK_TILES], start=start, stop=not start)

            pe.wait_ge(zero_tile, 1)
            pe.wait_ge(prefix_read, 1)
            for b in range(BLOCKS):
                clear(b, True)
                with pe.Fori(b * BATCHES // 2, (b + 1) * BATCHES // 2) as g:
                    for q in range(2):
                        place(g * 2 + q, b, q)
                clear(b, False).then_inc(block_placed, 1)
            pe.wait_ge(w_lo, len(GROUPS))
            pe.wait_ge(dst_slots_ready, 1)
            for b in range(BLOCKS):
                last = nc.tensor.transpose(bank[4][0:BLOCK_TILES, b * P:(b + 1) * P],
                                           dst_slot[:, b * BLOCK_TILES:(b + 1) * BLOCK_TILES], ident[:, :])
            last.then_inc(dst_turned, 1)
            pe.wait_ge(bias_ready, 1)
            pe.wait_ge(pair_rel_ready, 1)
            pe.wait_ge(dst_row_ready, 1)

            def products(parts):
                (a_h, a_l), (b_h, b_l) = parts
                return (a_h, b_h), (a_l, b_h), (a_h, b_l)

            def step(at):
                older, newer = (at - 2).within(PAIRS), (at - 1).within(PAIRS)
                rel_of = {}
                if older or newer:
                    first = at - 2 if older else at - 1
                    _, values = nc.values_load_multi_w_load_instructions(
                        pair_rel[0:1, bass.ds(first.n, older + newer)], engines=[mybir.EngineType.PE], min_val=0, max_val=1)
                    rel_of = dict(zip(([2] if older else []) + ([1] if newer else []), values))
                k = at
                if k.within(PAIRS):
                    pe.wait_ge(normed, k.n + 1)
                    for h in range(KH):
                        for t in range(2):
                            c = h * PAIR + t * P
                            last = nc.tensor.transpose(B_T[k.slot(2)][:, c:c + P],
                                                       xn[:, k.slot(2), t, h * P:(h + 1) * P], ident[:, :])
                    last.then_inc(s_turned, 1)
                k = at - 1
                if k.within(PAIRS):
                    r = rel_of[1]
                    pe.wait_ge(s_ready, k.n + 1)
                    for m in range(KH):
                        ps = B_H[k.slot(2)][:, m * PAIR:(m + 1) * PAIR]
                        nc.tensor.matmul(ps, brel_parts[:, bass.ds(r * D + m * P, P)], ones16[:, :], start=True, stop=False)
                        todo = []
                        for kk in range(KH):
                            w = [relT[:, bass.ds(r * REL_W + (kk * 2 + s) * D + m * P, P)] for s in range(2)]
                            v = [t[:, k.slot(2), kk * PAIR:(kk + 1) * PAIR] for t in (s_hi, s_lo)]
                            todo += products((w, v))
                        for i, (lhs, rhs) in enumerate(todo):
                            last = nc.tensor.matmul(ps, lhs, rhs, start=False, stop=i == len(todo) - 1)
                    last.then_inc(h_done, 1)
                k = at - 2
                if k.within(PAIRS):
                    r = rel_of[2]
                    pe.wait_ge(h_ready, k.n + 1)
                    for t in range(2):
                        ps = B_M[k.slot(2)][:, t * D:(t + 1) * D]
                        nc.tensor.matmul(ps, ones16[:, 0:P], brel_parts[:, bass.ds(r * D, D)], start=True, stop=False)
                        todo = []
                        for kk in range(KH):
                            c = kk * PAIR + t * P
                            w = [relT[:, bass.ds(r * REL_W + (kk * 2 + s) * D, D)] for s in range(2)]
                            v = [u[:, k.slot(2), c:c + P] for u in (h_hi, h_lo)]
                            todo += products((v, w))
                        for i, (lhs, rhs) in enumerate(todo):
                            last = nc.tensor.matmul(ps, lhs, rhs, start=False, stop=i == len(todo) - 1)
                    last.then_inc(m_done, 1)
                k = at - 3
                if k.within(PAIRS):
                    pe.wait_ge(m_ready, k.n + 1)
                    pe.wait_ge(same_ready, k.n + 1)
                    wait_from(pe, summed_ready, k.n - 1)
                    s = k.slot(2)
                    for ps, todo in (
                        (B_G[s][:, 0:D], [(same[:, s, 0, :], m[:, s, 0:D]) for m in (m_hi, m_lo)]
                         + [(same[:, s, 1, :], m[:, s, D:2 * D]) for m in (m_hi, m_lo)]),
                        (B_G[s][:, D:2 * D], [(same[:, s, 2, :], m[:, s, D:2 * D]) for m in (m_hi, m_lo)]),
                    ):
                        for i, (lhs, rhs) in enumerate(todo):
                            last = nc.tensor.matmul(ps, lhs, rhs, start=i == 0, stop=i == len(todo) - 1)
                    last.then_inc(sum_done, 1)

            run_steps(pe, 0, last=PAIRS + 3, step=step, **EDGE_RUN)

            pe.wait_ge(summed_ready, PAIRS)

            def chunk(k, c):
                wait_from(pe, gate_ready, k.n * CHUNKS + c - 2)
                if c == 0:
                    pe.wait_ge(a_ready, k.n + 1)
                todo = []
                for kk in range(KH):
                    w = [ihT[:, kk, s, c * P:(c + 1) * P] for s in range(2)]
                    v = [t[:, k.slot(2), kk, :] for t in (a_hi, a_lo)]
                    todo += products((w, v))
                for i, (lhs, rhs) in enumerate(todo):
                    last = nc.tensor.matmul(N_C[c % 3][:, :], lhs, rhs, start=i == 0, stop=i == len(todo) - 1)
                last.then_inc(chunk_done, 1)

            def turn_agg(k):
                pe.wait_ge(agg_loaded[k.slot(2)], 16 * (k.turn(2) + 1))
                wait_from(pe, a_ready, k.n)
                for h in range(KH):
                    for t in range(UT):
                        last = nc.tensor.transpose(N_T[h][:, t * P:(t + 1) * P],
                                                   agg_in[:, k.slot(2), t, h * P:(h + 1) * P], ident[:, :])
                last.then_inc(a_turned, 1)

            def mlp1(k):
                pe.wait_ge(hn_ready, (k.n + 1) * KH)
                wait_from(pe, x2_f_ready, k.n)
                todo = []
                for kk in range(KH):
                    w = [w1T[:, s, kk * RH:(kk + 1) * RH] for s in range(2)]
                    v = [t[:, k.slot(2), kk, :] for t in (hn_hi, hn_lo)]
                    todo += products((w, v))
                for i, (lhs, rhs) in enumerate(todo):
                    last = nc.tensor.matmul(N_X[:, :], lhs, rhs, start=i == 0, stop=i == len(todo) - 1)
                last.then_inc(x1_done, 1)

            def mlp2(k):
                pe.wait_ge(x1_ready, k.n + 1)
                todo = products(([w2T[:, s, :] for s in range(2)], (x1_hi[:, :], x1_lo[:, :])))
                for i, (lhs, rhs) in enumerate(todo):
                    last = nc.tensor.matmul(N_X[:, :], lhs, rhs, start=i == 0, stop=i == len(todo) - 1)
                last.then_inc(x2_done, 1)

            def mlp3(k):
                pe.wait_ge(x2_ready, k.n + 1)
                wait_from(pe, y_ready, k.n)
                for t in range(UT):
                    v = [u[:, t * P:(t + 1) * P] for u in (x2_hi, x2_lo)]
                    todo = products((v, [w3T[:, s, :] for s in range(2)]))
                    for i, (lhs, rhs) in enumerate(todo):
                        last = nc.tensor.matmul(N_Y[t // 2][:, (t % 2) * D:(t % 2 + 1) * D], lhs, rhs,
                                                start=i == 0, stop=i == len(todo) - 1)
                last.then_inc(y_done, 1)

            def node_step(at):
                now, last, older, after = (at.within(UNITS), (at - 1).within(UNITS), (at - 2).within(UNITS),
                                           (at + 1).within(UNITS))
                if now:
                    chunk(at, 0)
                    chunk(at, 1)
                if older:
                    mlp3(at - 2)
                if now:
                    chunk(at, 2)
                if last:
                    mlp1(at - 1)
                if now:
                    chunk(at, 3)
                if after:
                    turn_agg(at + 1)
                if now:
                    chunk(at, 4)
                if last:
                    mlp2(at - 1)
                if now:
                    chunk(at, 5)

            run_steps(pe, -1, last=UNITS + 2, step=node_step, **NODE_RUN)


_INS = ['x', 'src', 'dst', 'edge_type_2', 'L0_gnn_W_rel', 'L0_gnn_b_rel', 'L0_gnn_W_ih', 'L0_gnn_b_ih',
        'L0_gnn_b_hh', 'L0_gnn_W1', 'L0_gnn_b1', 'L0_gnn_W2', 'L0_gnn_b2', 'L0_gnn_W3', 'L0_gnn_b3']


def kernel(**inputs):
    import numpy as _np
    import concourse.bacc as _bacc
    from concourse import mybir as _mybir
    from concourse.bass_utils import run_bass_kernel_spmd as _run

    nc = _bacc.Bacc("TRN2", target_bir_lowering=False, num_devices=1)
    arrays, args = {}, []
    for name in _INS:
        a = _np.ascontiguousarray(inputs[name])
        arrays[f"in_{name}"] = a
        args.append(nc.dram_tensor(f"in_{name}", a.shape, _mybir.dt.from_np(a.dtype), kind="ExternalInput").ap())
    args.append(nc.dram_tensor("out_0", (NODES, D), _mybir.dt.float32, kind="ExternalOutput").ap())
    build(nc, *args)
    r = _run(nc, [arrays], core_ids=[0])
    return r.results[0]["out_0"]
```
